# Optimizing a Trainium2 kernel written in Bass

```python
import numpy as np
import jax
import jax.numpy as jnp

def _softmax(x, axis=-1):
    return jax.nn.softmax(x, axis=axis)

def _gelu(x):
    return jax.nn.gelu(x, approximate=True)

def _silu(x):
    return jax.nn.silu(x)

def _sigmoid(x):
    return jax.nn.sigmoid(x)

def _layernorm(x, axis=-1, eps=1e-05):
    m = jnp.mean(x, axis=axis, keepdims=True)
    v = jnp.var(x, axis=axis, keepdims=True)
    return (x - m) / jnp.sqrt(v + eps)

def _scatter_add(tgt, idx, src, axis=0):
    return tgt.at[idx].add(src)

def _segment_sum(src, seg, n):
    return jax.ops.segment_sum(src, seg, n)
kernel_name = 'mk_gnn_preln_d2_gnn_r8_896af3'

def setup_inputs(seed: int=0):
    np.random.seed(seed)
    _w = jnp.asarray

    def _rec_inputs():
        import jax
        import jax.numpy as jnp
        _gk = jax.random.key(seed)
        x = -8.776e-05 + 1 * jax.random.normal(jax.random.fold_in(_gk, 1), (1250, 512), jnp.float32)
        _s = jax.random.randint(jax.random.fold_in(_gk, 2), (20000,), 0, 1250, jnp.int32)
        _d = jax.random.randint(jax.random.fold_in(_gk, 3), (20000,), 0, 1250, jnp.int32)
        _loop = jnp.arange(1250, dtype=jnp.int32)
        src = jnp.concatenate([_s, _d, _loop])
        dst = jnp.concatenate([_d, _s, _loop])
        _o = jnp.argsort(dst, stable=True)
        src = src[_o]
        dst = dst[_o]
        edge_weight = jax.random.uniform(jax.random.fold_in(_gk, 13), (41250,), jnp.float32, 0.0, 0.999998)
        return (x, src, dst, edge_weight)
    x, src, dst, edge_weight = _rec_inputs()

    def _L0_gnn_setup():
        import jax, jax.numpy as jnp
        import numpy as np
        N_NODES = 1250
        N_EDGES = 20000
        D_FEAT = 512
        OUT_CH = 512
        key = jax.random.key(seed)
        k1, k2, k3, k4 = jax.random.split(key, 4)
        x = jax.random.normal(k1, (N_NODES, D_FEAT), dtype=jnp.float32)
        edge_index = jax.random.randint(k2, (N_EDGES, 2), 0, N_NODES, dtype=jnp.int64)
        W = jax.random.normal(k3, (OUT_CH, 2 * D_FEAT), dtype=jnp.float32) / np.sqrt(2 * D_FEAT)
        b = jax.random.normal(k4, (OUT_CH,), dtype=jnp.float32) * 0.01
        return {'x': x, 'edge_index': edge_index, 'num_local_nodes': N_NODES, 'W': W, 'b': b}
    _L0_gnn_all = _L0_gnn_setup()
    _L0_gnn_in = {k: v for k, v in _L0_gnn_all.items() if k in ('W', 'b')}
    del _L0_gnn_all

    def _L1_gnn_setup():
        import jax, jax.numpy as jnp
        import numpy as np
        N_NODES = 12500
        N_EDGES = 50000
        IN_FT = 512
        OUT_FT = 512
        key = jax.random.key(seed)
        k_feat, k_ei, k_ew, k_w, k_a = jax.random.split(key, 5)
        feat = jax.random.normal(k_feat, (N_NODES, IN_FT), dtype=jnp.float32)
        edge_index = jax.random.randint(k_ei, (2, N_EDGES), 0, N_NODES, dtype=jnp.int64)
        edge_weight = jax.random.uniform(k_ew, (N_EDGES,), dtype=jnp.float32)
        bound = float(np.sqrt(6.0 / (IN_FT + OUT_FT)))
        W = jax.random.uniform(k_w, (OUT_FT, IN_FT), dtype=jnp.float32, minval=-bound, maxval=bound)
        alpha = jnp.array(0.25, dtype=jnp.float32)
        return {'feat': feat, 'edge_index': edge_index, 'edge_weight': edge_weight, 'num_nodes': N_NODES, 'W': W, 'alpha': alpha}
    _L1_gnn_all = _L1_gnn_setup()
    _L1_gnn_in = {k: v for k, v in _L1_gnn_all.items() if k in ('W', 'alpha')}
    del _L1_gnn_all
    return {'x': x, 'src': src, 'dst': dst, 'edge_weight': edge_weight, 'L0_gnn_W': _L0_gnn_in['W'], 'L0_gnn_b': _L0_gnn_in['b'], 'L1_gnn_W': _L1_gnn_in['W'], 'L1_gnn_alpha': _L1_gnn_in['alpha']}

def reference(x, src, dst, edge_weight, L0_gnn_W, L0_gnn_b, L1_gnn_W, L1_gnn_alpha):
    import jax
    import jax.numpy as jnp

    def _L0_gnn_ref(x, edge_index, num_local_nodes, W, b):
        import jax, jax.numpy as jnp
        import numpy as np
        N_NODES = 1250
        N_EDGES = 20000
        D_FEAT = 512
        OUT_CH = 512
        src = edge_index[:, 0]
        tgt = edge_index[:, 1]
        x_i = x[src]
        x_j = x[tgt]
        x_ij = jnp.concatenate([x_i, x_j], axis=1)
        m_ij = jax.nn.relu(x_ij @ W.T + b)
        out = jax.ops.segment_sum(m_ij, src, num_segments=num_local_nodes)
        return out

    def _L1_gnn_ref(feat, edge_index, edge_weight, num_nodes, W, alpha):
        import jax, jax.numpy as jnp
        import numpy as np
        N_NODES = 12500
        N_EDGES = 50000
        IN_FT = 512
        OUT_FT = 512
        h = jnp.einsum('ni,oi->no', feat, W)
        row, col = (edge_index[0], edge_index[1])
        msgs = h[row] * edge_weight[:, None]
        out = jax.ops.segment_sum(msgs, col, num_segments=num_nodes)
        return jnp.where(out >= 0, out, alpha * out)
    edge_index = jnp.stack([src, dst])
    edge_index_t = jnp.stack([src, dst], axis=1)
    h = jnp.maximum(_layernorm(x, axis=-1), 0.0)
    x = x + _L0_gnn_ref(h, edge_index_t, 1250, L0_gnn_W, L0_gnn_b)
    h = jnp.maximum(_layernorm(x, axis=-1), 0.0)
    x = x + _L1_gnn_ref(h, edge_index, edge_weight, 1250, L1_gnn_W, L1_gnn_alpha)
    return x

_drawn_inputs = setup_inputs


def setup_inputs(seed=0):
    import zlib

    import numpy as np

    out = dict(_drawn_inputs(seed))
    spreads = {}
    factors = {'L0_gnn_b': 3.811}
    for name, (base, spread) in spreads.items():
        noise = np.random.default_rng([zlib.crc32(name.encode()), seed]).standard_normal(out[name].shape)
        drawn = base * np.exp(spread * noise) if base else spread * noise
        out[name] = jnp.asarray(drawn.astype(out[name].dtype))
    for name, factor in factors.items():
        out[name] = (out[name] * factor).astype(out[name].dtype)
    return out
```

```python
from contextlib import ExitStack

import concourse.bass as bass
from concourse import mybir

ALU = mybir.AluOpType
ACT = mybir.ActivationFunctionType
AX = mybir.AxisListType
F32 = mybir.dt.float32
F32R = mybir.dt.float32r
BF16 = mybir.dt.bfloat16
I32 = mybir.dt.int32

P = 128
N = 1250
D = 512
E = 41250
BN = 125
NBLK = N // BN
NBKT = NBLK * NBLK
EROWS = 125
ECOLS = E // EROWS
TILE = 128
GRP = 4
MAXT = (E + (TILE - 1) * NBKT) // TILE + NBLK * (GRP - 1)
NGRP = MAXT // GRP
NT = NGRP * GRP
FIELDS = 4
CCOL = 15
NCHUNK = ECOLS // CCOL
KC = D // P
OHW = BN + 1
MAGIC = 12582912.0
EPS = 1e-5
assert EROWS * ECOLS == E and NCHUNK * CCOL == ECOLS and NCHUNK % 2 == 0 and NGRP % 2 == 0


def build(nc, x, src, dst, edge_weight, w0, b0, w1, alpha, out):
    table_dram = nc.dram_tensor("edge_table", [P * NT, FIELDS], F32).ap()
    with ExitStack() as top:
        def sb(name, shape, dt, scope=top, side="left"):
            return scope.enter_context(nc.sbuf_tensor(name, shape, dt, side=side))

        def sem(name):
            return top.enter_context(nc.semaphore(name))

        S = sb("S", [P, NBLK, D], F32)
        ident = sb("ident", [P, P], F32)
        iota = sb("iota", [P, NT], F32)
        table = sb("table", [P, NT, FIELDS], F32)
        tile_dst = sb("tile_dst", [1, NT], I32)
        tile_bkt = sb("tile_bkt", [1, NT], I32)
        group_src = sb("group_src", [1, NGRP], I32)
        alpha_t = sb("alpha_t", [P, 1], F32)
        eps_t = sb("eps_t", [P, 1], F32)
        neg_mean = sb("neg_mean", [P, NBLK], F32)
        rstd = sb("rstd", [P, NBLK], F32)
        shift = sb("shift", [P, NBLK], F32)

        scope_ab = ExitStack()
        a_hi = sb("a_hi", [BN, NBLK * D], F32R, scope_ab, "right")
        a_lo = sb("a_lo", [BN, NBLK * D], F32R, scope_ab, "right")
        b_hi = sb("b_hi", [BN, NBLK * D], F32R, scope_ab, "right")
        b_lo = sb("b_lo", [BN, NBLK * D], F32R, scope_ab, "right")

        with ExitStack() as scope:
            def sb1(name, shape, dt):
                return sb(name, shape, dt, scope)

            src_i = sb1("src_i", [EROWS, ECOLS], I32)
            dst_i = sb1("dst_i", [EROWS, ECOLS], I32)
            weight = sb1("weight", [EROWS, ECOLS], F32)
            node_f = sb1("node_f", [EROWS, 2, ECOLS], F32)
            blk_a = sb1("blk_a", [EROWS, 2, ECOLS], F32)
            blk_b = sb1("blk_b", [EROWS, 2, ECOLS], F32)
            weight_hi = sb1("weight_hi", [EROWS, ECOLS], F32R)
            bucket = sb1("bucket", [EROWS, ECOLS], F32)
            payload = sb1("payload", [EROWS, ECOLS, FIELDS], F32)
            onehot = [sb1(f"onehot{k}", [EROWS, CCOL, NBKT], BF16) for k in range(2)]
            ident_b = sb1("ident_b", [P, P], BF16)
            minus_ident = sb1("minus_ident", [P, P], F32R)
            before = sb1("before", [P, P], F32)
            ones = sb1("ones", [P, P], F32)
            row_count = sb1("row_count", [EROWS, NBKT], F32)
            zt = sb1("zt", [EROWS, NBKT], F32)
            tiles_of = sb1("tiles_of", [EROWS, NBKT], F32)
            tiles_to = sb1("tiles_to", [EROWS, NBKT], F32)
            tile_base = sb1("tile_base", [EROWS, NBKT], F32)
            blk_small = sb1("blk_small", [EROWS, 6, NBLK], F32)
            ones_row = sb1("ones_row", [EROWS, NBKT], F32)
            slot_next = [sb1(f"slot_next{k}", [EROWS, NBKT], F32) for k in range(2)]
            picked = sb1("picked", [EROWS, NBKT], F32)
            slot = [sb1(f"slot{k}", [EROWS, CCOL], F32) for k in range(2)]
            slot_tile = sb1("slot_tile", [EROWS, 3, CCOL], F32)
            stage_row = [sb1(f"stage_row{k}", [EROWS, CCOL], I32) for k in range(2)]
            stage_pay = [sb1(f"stage_pay{k}", [EROWS, CCOL, FIELDS], F32) for k in range(2)]
            started = sb1("started", [NBKT, NT], F32)
            bkt_small = sb1("bkt_small", [NBKT, 8], F32)
            w_in = sb1("w_in", [P, KC, 2 * D], F32)
            w0T = sb1("w0T", [P, 2 * KC, D], F32)
            bias_row = sb1("bias_row", [1, D], F32)
            h1 = [sb1(f"h1_{k}", [BN, D], F32) for k in range(2)]
            h1T = [sb1(f"h1T{k}", [P, KC, BN], F32) for k in range(2)]
            gate = sb1("gate", [P, 2], F32)
            sums = sb1("sums", [BN, 3, NBLK], F32)

            psum = scope.enter_context(nc.psum_tensor("psum1", [P, 8, 512], F32))
            count_ps = psum[0:EROWS, 0, 0:NBKT]
            total_ps = psum[0:EROWS, 0, 128:128 + NBKT]
            above_ps = psum[0:EROWS, 0, 256:256 + NBKT]
            base_col_ps = psum[0:NBKT, 0, 384:385]

            edges_in = sem("edges_in")
            weight_in = sem("weight_in")
            x_in = sem("x_in")
            w_loaded = sem("w_loaded")
            small_in = sem("small_in")
            consts = sem("consts")
            dconst = sem("dconst")
            pool_own = sem("pool_own")
            cleared = sem("cleared")
            cleared_dram = sem("cleared_dram")
            vstep = sem("vstep")
            payload_done = sem("payload_done")
            hot_ready = sem("hot_ready")
            hot_used = sem("hot_used")
            counted = sem("counted")
            count_out = sem("count_out")
            totals = sem("totals")
            base_ready = sem("base_ready")
            base_col = sem("base_col")
            started_ready = sem("started_ready")
            tables_ps = sem("tables_ps")
            slots_moved = sem("slots_moved")
            slot_found = sem("slot_found")
            slot_math = sem("slot_math")
            staged = sem("staged")
            chunk_taken = sem("chunk_taken")
            scattered = [sem("scattered0"), sem("scattered1")]
            table_in = sem("table_in")
            act_own = sem("act_own")
            std_ready = sem("std_ready")
            rstd_ready = sem("rstd_ready")
            tr_ready = sem("tr_ready")
            tr_out = sem("tr_out")
            h_ready = sem("h_ready")
            hT_ready = sem("hT_ready")
            ab_ps = sem("ab_ps")
            ab_hi_out = sem("ab_hi_out")
            ab_low = sem("ab_low")
            ab_out = sem("ab_out")

            with nc.Block() as block:
                @block.sync
                def _(sp):
                    sp.dma_start(src_i[:], src.rearrange("(p c) -> p c", p=EROWS)).then_inc(edges_in, 16)
                    sp.dma_start(dst_i[:], dst.rearrange("(p c) -> p c", p=EROWS)).then_inc(edges_in, 16)
                    sp.dma_start(weight[:], edge_weight.rearrange("(p c) -> p c", p=EROWS)).then_inc(weight_in, 16)
                    sp.dma_start(S[0:BN], x.rearrange("(b p) d -> p b d", p=BN)).then_inc(x_in, 16)
                    sp.dma_start(w_in[:], w0.rearrange("(o p) i -> p o i", p=P)).then_inc(w_loaded, 16)
                    sp.dma_start(bias_row[:], b0.rearrange("(a d) -> a d", a=1)).then_inc(small_in, 16)
                    sp.dma_start(alpha_t[:], alpha.rearrange("(a d) -> a d", a=1).to_broadcast([P, 1])).then_inc(small_in, 16)
                    sp.wait_ge(cleared, 1)
                    sp.dma_start(table_dram.rearrange("(p t) f -> p (t f)", p=P),
                                 table.rearrange("p t f -> p (t f)")).then_inc(cleared_dram, 16)
                    for k in range(2):
                        sp.wait_ge(scattered[k], 16 * CCOL * (NCHUNK // 2))
                    sp.dma_start(table.rearrange("p t f -> p (t f)"),
                                 table_dram.rearrange("(p t) f -> p (t f)", p=P)).then_inc(table_in, 16)
                    sp.wait_ge(table_in, 16)
                    sp.wait_ge(small_in, 32)

                @block.gpsimd
                def _(pool):
                    pool.iota(iota[:], [[1, NT]], base=0, channel_multiplier=0,
                              allow_small_or_imprecise_dtypes=True).then_inc(consts, 1)
                    pool.memset(table[:], -1.0).then_inc(cleared, 1)
                    pool.memset(ones[:], 1.0).then_inc(pool_own, 1)
                    pool.wait_ge(pool_own, 1)
                    pool.affine_select(out=ident[:], in_=ones[:], compare_op=ALU.is_equal, fill=0.0, base=0,
                                       pattern=[[-1, P]], channel_multiplier=1).then_inc(consts, 1)
                    pool.affine_select(out=before[:], in_=ones[:], compare_op=ALU.is_gt, fill=0.0, base=0,
                                       pattern=[[1, P]], channel_multiplier=-1).then_inc(consts, 1)
                    pool.iota(bkt_small[:, 0:1], [[0, 1]], base=0, channel_multiplier=1,
                              allow_small_or_imprecise_dtypes=True).then_inc(consts, 1)
                    pool.wait_ge(cleared_dram, 16)
                    with pool.Fori(0, NCHUNK // 2) as it:
                        for k in range(2):
                            pool.wait_ge(staged, it * 4 + 2 * (k + 1))
                            pool.tensor_tensor(gate[:, k:k + 1], ones[:, 0:1], ones[:, 1:2],
                                               ALU.add).then_inc(chunk_taken, 1)
                            for c in range(CCOL):
                                pool.indirect_dma_start(
                                    table_dram[:, :], bass.IndirectOffsetOnAxis(ap=stage_row[k][:, c:c + 1], axis=0),
                                    stage_pay[k][:, c, :], None).then_inc(scattered[k], 16)

                @block.vector
                def _(dve):
                    steps = [0]

                    def own(ins):
                        steps[0] += 1
                        ins.then_inc(vstep, 1)
                        dve.wait_ge(vstep, steps[0])

                    dve.memset(eps_t[:], EPS).then_inc(dconst, 1)
                    dve.memset(ones_row[:], 1.0).then_inc(dconst, 1)
                    dve.wait_ge(edges_in, 32)
                    own(dve.tensor_copy(node_f[:, 0, :], src_i[:]))
                    own(dve.tensor_copy(node_f[:, 1, :], dst_i[:]))
                    own(dve.tensor_scalar(blk_a[:], node_f[:], -(BN - 1) / 2, 1.0 / BN, ALU.add, ALU.mult))
                    own(dve.tensor_scalar(blk_b[:], blk_a[:], MAGIC, None, ALU.add))
                    own(dve.tensor_scalar(blk_a[:], blk_b[:], -MAGIC, None, ALU.add))
                    own(dve.scalar_tensor_tensor(out=bucket[:], in0=blk_a[:, 0, :], scalar=float(NBLK),
                                                 in1=blk_a[:, 1, :], op0=ALU.mult, op1=ALU.add))
                    dve.wait_ge(consts, 1)
                    for c in range(NCHUNK):
                        if c >= 2:
                            dve.wait_ge(hot_used, c - 1)
                        dve.tensor_tensor(onehot[c % 2][:],
                                          bucket[:, c * CCOL:(c + 1) * CCOL].unsqueeze(2).to_broadcast([EROWS, CCOL, NBKT]),
                                          iota[0:EROWS, 0:NBKT].unsqueeze(1).to_broadcast([EROWS, CCOL, NBKT]),
                                          ALU.is_equal).then_inc(hot_ready, 1)
                    for k in range(2):
                        own(dve.scalar_tensor_tensor(out=payload[:, :, k], in0=blk_a[:, k, :], scalar=-float(BN),
                                                     in1=node_f[:, k, :], op0=ALU.mult, op1=ALU.add))
                    dve.wait_ge(weight_in, 16)
                    own(dve.tensor_copy(weight_hi[:], weight[:]))
                    own(dve.tensor_copy(payload[:, :, 2], weight_hi[:].bitcast(F32)))
                    own(dve.tensor_tensor(payload[:, :, 3], weight[:], weight_hi[:].bitcast(F32), ALU.subtract))
                    dve.wait_ge(counted, 1)
                    dve.tensor_copy(row_count[:], count_ps).then_inc(count_out, 1)
                    dve.wait_ge(totals, 1)
                    own(dve.tensor_scalar(zt[:], total_ps, (TILE - 1) / 2, 1.0 / TILE, ALU.add, ALU.mult))
                    own(dve.tensor_scalar(tiles_to[:], zt[:], MAGIC, None, ALU.add))
                    own(dve.tensor_scalar(tiles_of[:], tiles_to[:], -MAGIC, None, ALU.add))
                    in_blk, grp_a, grp_b, grp_to, start = (blk_small[:, k, :] for k in range(5))
                    own(dve.tensor_reduce(in_blk, tiles_of.rearrange("p (s d) -> p s d", s=NBLK), AX.X, ALU.add))
                    own(dve.tensor_scalar(grp_a, in_blk, (GRP - 1) / 2, 1.0 / GRP, ALU.add, ALU.mult))
                    own(dve.tensor_scalar(grp_b, grp_a, MAGIC, None, ALU.add))
                    own(dve.tensor_scalar(grp_a, grp_b, -MAGIC, None, ALU.add))
                    own(dve.tensor_tensor_scan(grp_to, ones_row[:, 0:NBLK], grp_a, 0.0, ALU.mult, ALU.add))
                    own(dve.tensor_tensor(grp_b, grp_to, grp_a, ALU.subtract))
                    own(dve.tensor_tensor_scan(tiles_to[:], ones_row[:], tiles_of[:], 0.0, ALU.mult, ALU.add))
                    own(dve.tensor_tensor(zt[:], tiles_to[:], tiles_of[:], ALU.subtract))
                    first_of_blk = zt.rearrange("p (s d) -> p s d", s=NBLK)[:, :, 0]
                    own(dve.scalar_tensor_tensor(out=start, in0=grp_b, scalar=float(GRP), in1=first_of_blk,
                                                 op0=ALU.mult, op1=ALU.subtract))
                    own(dve.tensor_tensor(tile_base.rearrange("p (s d) -> p s d", s=NBLK),
                                          zt.rearrange("p (s d) -> p s d", s=NBLK),
                                          start.unsqueeze(2).to_broadcast([EROWS, NBLK, NBLK]), ALU.add))
                    dve.scalar_tensor_tensor(out=slot_next[0][:], in0=tile_base[:], scalar=float(TILE), in1=above_ps,
                                             op0=ALU.mult, op1=ALU.add).then_inc(slots_moved, 1)
                    dve.memset(picked[:], 0.0).then_inc(slot_found, 1)
                    dve.wait_ge(std_ready, 1)
                    dve.reciprocal(rstd[0:BN, :], sums[:, 2, :]).then_inc(rstd_ready, 1)
                    dve.wait_ge(rstd_ready, 1)
                    dve.tensor_tensor(shift[0:BN, :], neg_mean[0:BN, :], rstd[0:BN, :], ALU.mult).then_inc(rstd_ready, 1)

                    def slots_of_chunk(it, k, first):
                        for c in range(CCOL):
                            n = it * (2 * CCOL) + (k * CCOL + c)
                            col = bucket[:, c + k * CCOL:c + k * CCOL + 1] if first else \
                                bucket[:, bass.ds(it * (2 * CCOL) + (k * CCOL + c), 1)]
                            now, then = slot_next[(k * CCOL + c) % 2], slot_next[(k * CCOL + c + 1) % 2]
                            dve.wait_ge(slots_moved, n + 1)
                            dve.wait_ge(slot_found, n + 1)
                            if c == 0 and not (first and k == 0):
                                dve.wait_ge(slot_math, (it * 2 + k) * 4)
                            dve.scalar_tensor_tensor(out=picked[:], in0=iota[0:EROWS, 0:NBKT], scalar=col, in1=now[:],
                                                     op0=ALU.is_equal, op1=ALU.mult,
                                                     accum_out=slot[k][:, c:c + 1]).then_inc(slot_found, 1)
                            dve.scalar_tensor_tensor(out=then[:], in0=iota[0:EROWS, 0:NBKT], scalar=col, in1=now[:],
                                                     op0=ALU.is_equal, op1=ALU.add).then_inc(slots_moved, 1)
                        base = (it * 2 + k) * 4
                        whole, tile_no, lane = (slot_tile[:, i, :] for i in range(3))
                        dve.wait_ge(slot_found, it * (2 * CCOL) + (k + 1) * CCOL + 1)
                        if not first:
                            dve.wait_ge(chunk_taken, it * 2 + (k - 1))
                            dve.wait_ge(scattered[k], it * (16 * CCOL))
                        if not (first and k == 0):
                            dve.wait_ge(staged, (it * 2 + k) * 2)
                        dve.tensor_scalar(whole, slot[k][:], -(TILE - 1) / 2, 1.0 / TILE, ALU.add, ALU.mult).then_inc(slot_math, 1)
                        dve.wait_ge(slot_math, base + 1)
                        dve.tensor_scalar(lane, whole, MAGIC, None, ALU.add).then_inc(slot_math, 1)
                        dve.wait_ge(slot_math, base + 2)
                        dve.tensor_scalar(tile_no, lane, -MAGIC, None, ALU.add).then_inc(slot_math, 1)
                        dve.wait_ge(slot_math, base + 3)
                        dve.scalar_tensor_tensor(out=lane, in0=tile_no, scalar=-float(TILE), in1=slot[k][:],
                                                 op0=ALU.mult, op1=ALU.add).then_inc(slot_math, 1)
                        dve.wait_ge(slot_math, base + 4)
                        dve.scalar_tensor_tensor(out=stage_row[k][:], in0=lane, scalar=float(NT), in1=tile_no,
                                                 op0=ALU.mult, op1=ALU.add).then_inc(staged, 1)
                        pay = payload[:, k * CCOL:(k + 1) * CCOL, :] if first else \
                            payload[:, bass.ds(it * (2 * CCOL) + k * CCOL, CCOL), :]
                        dve.tensor_copy(stage_pay[k][:], pay).then_inc(staged, 1)

                    slots_of_chunk(0, 0, True)
                    slots_of_chunk(0, 1, True)
                    with dve.Fori(1, NCHUNK // 2) as it:
                        slots_of_chunk(it, 0, False)
                        slots_of_chunk(it, 1, False)

                    dve.wait_ge(consts, 4)
                    dve.wait_ge(base_col, 1)
                    n_bkt, t1, t2, t3, src_start, col_base, dst_coef, all_one = (bkt_small[:, i:i + 1] for i in range(8))
                    own(dve.tensor_copy(col_base, base_col_ps))
                    own(dve.tensor_scalar(started[:], iota[0:NBKT, :], col_base, None, ALU.is_ge))
                    own(dve.tensor_scalar(t1, n_bkt, -(NBLK - 1) / 2, 1.0 / NBLK, ALU.add, ALU.mult))
                    own(dve.tensor_scalar(t2, t1, MAGIC, None, ALU.add))
                    own(dve.tensor_scalar(t3, t2, -MAGIC, -float(NBLK), ALU.add, ALU.mult))
                    own(dve.tensor_tensor(t1, n_bkt, t3, ALU.add))
                    own(dve.tensor_scalar(src_start, t1, 0.0, None, ALU.is_equal))
                    own(dve.tensor_scalar(dst_coef, src_start, -float(NBLK), 1.0, ALU.mult, ALU.add))
                    dve.memset(all_one, 1.0).then_inc(started_ready, 1)
                    dve.wait_ge(tables_ps, 1)
                    own(dve.tensor_scalar(tile_dst[:], psum[0:1, 1, 0:NT], float(NBLK - 1), None, ALU.add))
                    own(dve.tensor_scalar(group_src[:], psum[0:1, 2, 0:NGRP], -1.0, None, ALU.add))
                    own(dve.tensor_scalar(tile_bkt[:], psum[0:1, 3, 0:NT], -1.0, None, ALU.add))

                @block.tensor
                def _(pe):
                    pe.wait_ge(hot_ready, 1)
                    pe.wait_ge(ab_out, 1)
                    for c in range(NCHUNK):
                        pe.wait_ge(hot_ready, c + 1)
                        for k in range(CCOL):
                            mm = pe.matmul(count_ps, ident_b[0:EROWS, 0:EROWS], onehot[c % 2][:, k, :],
                                           start=(c == 0 and k == 0), stop=(c == NCHUNK - 1 and k == CCOL - 1))
                        mm.then_inc(counted if c == NCHUNK - 1 else hot_used, 1)
                    pe.wait_ge(count_out, 1)
                    pe.wait_ge(consts, 3)
                    pe.matmul(total_ps, ones[0:EROWS, 0:EROWS], row_count[:], start=True, stop=True)
                    pe.matmul(above_ps, before[0:EROWS, 0:EROWS], row_count[:], start=True, stop=True).then_inc(totals, 1)
                    pe.wait_ge(w_loaded, 16)
                    for i in range(2 * KC):
                        if i >= 2:
                            pe.wait_ge(tr_out, i - 1)
                        for o in range(KC):
                            mm = pe.transpose(psum[:, 4 + i % 2, o * P:(o + 1) * P], w_in[:, o, i * P:(i + 1) * P], ident[:])
                        mm.then_inc(tr_ready, 1)
                    pe.wait_ge(small_in, 32)
                    for b in range(NBLK):
                        pe.wait_ge(h_ready, b + 1)
                        pe.wait_ge(tr_out, 2 * KC + b - 1)
                        for c in range(KC):
                            mm = pe.transpose(psum[:, 4 + b % 2, c * BN:(c + 1) * BN], h1[b % 2][:, c * P:(c + 1) * P],
                                              ident[0:BN, 0:BN])
                        mm.then_inc(tr_ready, 1)
                        pe.wait_ge(tr_out, 2 * KC + b + 1)
                        for m in range(2):
                            if b >= 1:
                                pe.wait_ge(ab_out, 2 * b + m)
                            ps = psum[0:BN, 6 + m, :]
                            if m == 0:
                                pe.matmul(ps, ones[0:1, 0:BN], bias_row[:], start=True, stop=False)
                            for c in range(KC):
                                mm = pe.matmul(ps, h1T[b % 2][:, c, :], w0T[:, m * KC + c, :],
                                               start=(m == 1 and c == 0), stop=(c == KC - 1))
                            mm.then_inc(ab_ps, 1)
                        for m in range(2):
                            pe.wait_ge(ab_hi_out, 2 * b + m + 1)
                            pe.matmul(psum[0:BN, 6 + m, :], minus_ident[0:BN, 0:BN],
                                      (a_hi, b_hi)[m][:, b * D:(b + 1) * D], start=False, stop=True,
                                      skip_group_check=True).then_inc(ab_low, 1)
                    pe.wait_ge(slots_moved, 1)
                    pe.matmul(base_col_ps, tile_base[0:1, :], ones[0:1, 0:1], start=True, stop=True).then_inc(base_col, 1)
                    pe.wait_ge(started_ready, 1)
                    pe.matmul(psum[0:1, 1, 0:NT], bkt_small[:, 6:7], started[:], start=True, stop=True)
                    pe.matmul(psum[0:1, 2, 0:NGRP], bkt_small[:, 4:5], started[:, 0:NT:GRP], start=True, stop=True)
                    pe.matmul(psum[0:1, 3, 0:NT], bkt_small[:, 7:8], started[:], start=True, stop=True).then_inc(tables_ps, 1)

                @block.scalar
                def _(act):
                    act.wait_ge(consts, 3)
                    act.copy(ident_b[:], ident[:]).then_inc(ab_out, 1)
                    act.mul(minus_ident[:], ident[:], -1.0).then_inc(act_own, 1)
                    act.wait_ge(x_in, 16)
                    steps = 1
                    for b in range(NBLK):
                        act.wait_ge(act_own, steps)
                        act.activation(h1[0][:], S[0:BN, b, :], ACT.Identity, accum_out=sums[:, 0, b:b + 1]).then_inc(act_own, 1)
                        steps += 1
                    act.wait_ge(act_own, steps)
                    act.mul(neg_mean[0:BN, :], sums[:, 0, :], -1.0 / D).then_inc(act_own, 1)
                    steps += 1
                    for b in range(NBLK):
                        act.wait_ge(act_own, steps)
                        act.activation(h1[0][:], S[0:BN, b, :], ACT.Square, bias=neg_mean[0:BN, b:b + 1],
                                       accum_out=sums[:, 1, b:b + 1]).then_inc(act_own, 1)
                        steps += 1
                    act.wait_ge(act_own, steps)
                    act.wait_ge(dconst, 2)
                    act.activation(sums[:, 2, :], sums[:, 1, :], ACT.Sqrt, bias=eps_t[0:BN, :],
                                   scale=1.0 / D).then_inc(std_ready, 1)
                    for i in range(2 * KC):
                        act.wait_ge(tr_ready, i + 1)
                        act.copy(w0T[:, i, :], psum[:, 4 + i % 2, :]).then_inc(tr_out, 1)
                    act.wait_ge(rstd_ready, 2)

                    def normed(b):
                        if b >= 2:
                            act.wait_ge(tr_ready, 2 * KC + b - 1)
                        act.activation(h1[b % 2][:], S[0:BN, b, :], ACT.Relu, bias=shift[0:BN, b:b + 1],
                                       scale=rstd[0:BN, b:b + 1]).then_inc(h_ready, 1)

                    normed(0)
                    for b in range(NBLK):
                        act.wait_ge(tr_ready, 2 * KC + b + 1)
                        if b >= 2:
                            act.wait_ge(ab_ps, 2 * b - 2)
                        act.copy(h1T[b % 2][:], psum[:, 4 + b % 2, 0:KC * BN].rearrange("p (c n) -> p c n", c=KC)).then_inc(tr_out, 1)
                        if b + 1 < NBLK:
                            normed(b + 1)
                        for m in range(2):
                            act.wait_ge(ab_ps, 2 * b + m + 1)
                            act.copy((a_hi, b_hi)[m][:, b * D:(b + 1) * D], psum[0:BN, 6 + m, :]).then_inc(ab_hi_out, 1)
                        for m in range(2):
                            act.wait_ge(ab_low, 2 * b + m + 1)
                            act.copy((a_lo, b_lo)[m][:, b * D:(b + 1) * D], psum[0:BN, 6 + m, :]).then_inc(ab_out, 1)

        scope = ExitStack()
        M = sb("M", [BN, NBKT, BN], F32, scope)
        hot = [sb(f"hot{k}", [P, 2, GRP, OHW], F32R, scope) for k in range(2)]
        hot_w = sb("hot_w", [P, 2, GRP, OHW], F32R, scope)
        turned_s = [sb(f"turned_s{k}", [BN, GRP * P], F32R, scope) for k in range(2)]
        turned_d = [sb(f"turned_d{k}", [BN, GRP * P], F32R, scope) for k in range(2)]
        msg_hi = [sb(f"msg_hi{k}", [P, D], F32R, scope) for k in range(GRP)]
        msg_lo = [sb(f"msg_lo{k}", [P, D], F32R, scope) for k in range(GRP)]

        psum_scope = ExitStack()
        edge_ps = [psum_scope.enter_context(nc.psum_tensor(f"edge_ps{k}", [P, D], F32)) for k in range(GRP)]
        turn_ps = psum_scope.enter_context(nc.psum_tensor("turn_ps", [BN, GRP * P], F32))
        node_ps = [psum_scope.enter_context(nc.psum_tensor(f"node_ps{k}", [BN, D], F32)) for k in range(2)]
        m_ps = psum_scope.enter_context(nc.psum_tensor("m_ps", [BN, GRP, P], F32))

        m_clear = sem("m_clear")
        hots = sem("hots")
        hots_w = sem("hots_w")
        turn_ready = sem("turn_ready")
        turned = sem("turned")
        edge_ready = sem("edge_ready")
        hi_ready = sem("hi_ready")
        lo_ready = sem("lo_ready")
        tile_summed = sem("tile_summed")
        m_ready = sem("m_ready")
        node_added = sem("node_added")
        m_added = sem("m_added")

        with nc.Block() as block:
            @block.gpsimd
            def _(pool):
                def group(g, k, first=False):
                    rows = table[:, bass.ds(g * GRP, GRP), :]
                    pool.wait_ge(hots, g + 1)
                    if not first:
                        pool.wait_ge(m_ready, g)
                    for f in range(2):
                        pool.tensor_tensor(hot_w[:, f], hot[k][:, 1].bitcast(F32),
                                           rows[:, :, 2 + f:3 + f].to_broadcast([P, GRP, OHW]),
                                           ALU.mult).then_inc(hots_w, 1)

                group(0, 0, first=True)
                group(1, 1)
                with pool.Fori(1, NGRP // 2) as it:
                    group(it * 2, 0)
                    group(it * 2 + 1, 1)

            @block.tensor
            def _(pe):
                def turn(k, f):
                    for j in range(GRP):
                        mm = pe.transpose(turn_ps[:, j * P:(j + 1) * P], hot[k][:, f, j, 0:BN].bitcast(F32), ident[:])
                    mm.then_inc(turn_ready, 1)

                def sum_tile(g, j, k):
                    pe.wait_ge(lo_ready, g * GRP + j + 1)
                    pe.matmul(node_ps[k][:], hot[k][:, 0, j, 0:BN], msg_hi[j][:], start=(j == 0), stop=False)
                    pe.matmul(node_ps[k][:], hot[k][:, 0, j, 0:BN], msg_lo[j][:], start=False,
                              stop=(j == GRP - 1)).then_inc(tile_summed, 1)

                def weights(g, k):
                    pe.wait_ge(hots_w, g * 2 + 2)
                    for j in range(GRP):
                        for f in range(2):
                            mm = pe.matmul(m_ps[:, j, 0:OHW], hot[k][:, 0, j, 0:BN], hot_w[:, f, j, :],
                                           start=(f == 0), stop=(f == 1))
                    mm.then_inc(m_ready, 1)

                def group(g, k, first=False, second=False, last=False):
                    src_blk = pe.value_load(group_src[0:1, bass.ds(g, 1)], min_val=0, max_val=NBLK - 1)
                    dst_blk = [pe.value_load(tile_dst[0:1, bass.ds(g * GRP + j, 1)], min_val=0, max_val=NBLK - 1)
                               for j in range(GRP)]
                    for j in range(GRP):
                        if not first:
                            pe.wait_ge(lo_ready, g * GRP + j + 1 - GRP)
                        if j == 0:
                            pe.wait_ge(turned, g * 2 + 2)
                        ts, td = turned_s[k][:, j * P:(j + 1) * P], turned_d[k][:, j * P:(j + 1) * P]
                        pe.matmul(edge_ps[j][:], ts, a_hi[:, bass.ds(src_blk * D, D)], start=True, stop=False)
                        pe.matmul(edge_ps[j][:], ts, a_lo[:, bass.ds(src_blk * D, D)], start=False, stop=False)
                        pe.matmul(edge_ps[j][:], td, b_hi[:, bass.ds(dst_blk[j] * D, D)], start=False, stop=False)
                        pe.matmul(edge_ps[j][:], td, b_lo[:, bass.ds(dst_blk[j] * D, D)], start=False,
                                  stop=True).then_inc(edge_ready, 1)
                        if j == 2 and not last:
                            pe.wait_ge(hots, g + 2)
                            turn(1 - k, 0)
                        if j == 3 and not last:
                            pe.wait_ge(turned, g * 2 + 3)
                            turn(1 - k, 1)
                        if j < 2 and not first:
                            sum_tile(g - 1, j + 2, 1 - k)
                        if j >= 2:
                            if j == 2 and not (first or second):
                                pe.wait_ge(node_added, g - 1)
                            sum_tile(g, j - 2, k)
                    if not first:
                        pe.wait_ge(m_added, g * GRP)
                    weights(g, k)

                pe.wait_ge(hots, 1)
                turn(0, 0)
                pe.wait_ge(turned, 1)
                turn(0, 1)
                group(0, 0, first=True)
                group(1, 1, second=True)
                with pe.Fori(1, NGRP // 2 - 1) as it:
                    group(it * 2, 0)
                    group(it * 2 + 1, 1)
                group(NGRP - 2, 0)
                group(NGRP - 1, 1, last=True)
                sum_tile(NGRP - 1, 2, 1)
                sum_tile(NGRP - 1, 3, 1)

            @block.scalar
            def _(act):
                def group(g, k, first=False, last=False):
                    for j in range(GRP):
                        act.wait_ge(edge_ready, g * GRP + j + 1)
                        if not first:
                            act.wait_ge(tile_summed, g * GRP + j + 1 - GRP)
                        act.activation(msg_hi[j][:], edge_ps[j][:], ACT.Relu).then_inc(hi_ready, 1)
                        if j == 2 and not last:
                            act.wait_ge(turn_ready, g * 2 + 3)
                            act.copy(turned_s[1 - k][:], turn_ps[:]).then_inc(turned, 1)
                        if j == 3 and not last:
                            act.wait_ge(turn_ready, g * 2 + 4)
                            act.copy(turned_d[1 - k][:], turn_ps[:]).then_inc(turned, 1)

                act.wait_ge(turn_ready, 1)
                act.copy(turned_s[0][:], turn_ps[:]).then_inc(turned, 1)
                act.wait_ge(turn_ready, 2)
                act.copy(turned_d[0][:], turn_ps[:]).then_inc(turned, 1)
                group(0, 0, first=True)
                group(1, 1)
                with act.Fori(1, NGRP // 2 - 1) as it:
                    group(it * 2, 0)
                    group(it * 2 + 1, 1)
                group(NGRP - 2, 0)
                group(NGRP - 1, 1, last=True)

            @block.vector
            def _(dve):
                def add_sums(g, k, first=False):
                    blk = dve.value_load(group_src[0:1, bass.ds(g, 1)], min_val=0, max_val=NBLK - 1)
                    dve.wait_ge(tile_summed, g * GRP + GRP)
                    if not first:
                        dve.wait_ge(node_added, g)
                    rows = S.rearrange("p b d -> p (b d)")[0:BN, bass.ds(blk * D, D)]
                    dve.tensor_tensor(rows, rows, node_ps[k][:], ALU.add).then_inc(node_added, 1)

                def add_weights(g, first=False):
                    flat = M.rearrange("p b n -> p (b n)")
                    dve.wait_ge(m_ready, g + 1)
                    for j in range(GRP):
                        bkt = dve.value_load(tile_bkt[0:1, bass.ds(g * GRP + j, 1)], min_val=0, max_val=NBKT - 1)
                        if not (first and j == 0):
                            dve.wait_ge(m_added, g * GRP + j)
                        part = flat[:, bass.ds(bkt * BN, BN)]
                        dve.tensor_tensor(part, part, m_ps[:, j, 0:BN], ALU.add).then_inc(m_added, 1)

                def make_hots(g, k, first=False, second=False):
                    if not (first or second):
                        dve.wait_ge(tile_summed, (g - 1) * GRP)
                        dve.wait_ge(m_ready, g - 1)
                        dve.wait_ge(hots_w, (g - 1) * 2)
                    local = table[:, bass.ds(g * GRP, GRP), 0:2].rearrange("p t f -> p f t")
                    dve.tensor_tensor(hot[k][:], iota[:, 0:OHW].unsqueeze(1).unsqueeze(1).to_broadcast([P, 2, GRP, OHW]),
                                      local.unsqueeze(3).to_broadcast([P, 2, GRP, OHW]),
                                      ALU.is_equal).then_inc(hots, 1)

                def group(g, k, first=False, second=False, last=False):
                    for j in range(GRP):
                        dve.wait_ge(hi_ready, g * GRP + j + 1)
                        dve.scalar_tensor_tensor(out=msg_lo[j][:], in0=edge_ps[j][:], scalar=0.0,
                                                 in1=msg_hi[j][:].bitcast(F32), op0=ALU.max,
                                                 op1=ALU.subtract).then_inc(lo_ready, 1)
                        if j == 0 and not first:
                            add_weights(g - 1, first=second)
                        if j == 1:
                            if not last:
                                make_hots(g + 1, 1 - k, second=first)
                            if not first:
                                add_sums(g - 1, 1 - k, first=second)

                make_hots(0, 0, first=True)
                dve.memset(M[:], 0.0).then_inc(m_clear, 1)
                dve.wait_ge(m_clear, 1)
                group(0, 0, first=True)
                group(1, 1, second=True)
                with dve.Fori(1, NGRP // 2 - 1) as it:
                    group(it * 2, 0)
                    group(it * 2 + 1, 1)
                group(NGRP - 2, 0)
                group(NGRP - 1, 1, last=True)
                add_weights(NGRP - 1)
                add_sums(NGRP - 1, 1)

        psum_scope.close()
        scope_ab.close()
        with ExitStack() as tail:
            def sb3(name, shape, dt):
                return sb(name, shape, dt, tail, "right")

            G = sb3("G", [BN, NBLK, D], F32)
            w1_in = sb3("w1_in", [P, KC, D], F32)
            w1T = sb3("w1T", [P, KC, D], F32)
            h2 = [sb3(f"h2_{k}", [BN, D], F32) for k in range(2)]
            h2T = [sb3(f"h2T{k}", [P, KC, BN], F32) for k in range(2)]
            result = [sb3(f"result{k}", [BN, D], F32) for k in range(2)]
            neg_part = sb3("neg_part", [BN, D], F32)
            stats = sb3("stats", [BN, NBLK, nc.vector.BN_STATS_DIM], F32)
            mv = sb3("mv", [BN, NBLK, nc.vector.BN_AGGR_DIM], F32)
            std = sb3("std", [BN, NBLK], F32)
            psum = tail.enter_context(nc.psum_tensor("psum3", [P, 8, 512], F32))
            w1_loaded = sem("w1_loaded")
            stats_own = sem("stats_own")
            var_ready = sem("var_ready")
            std3 = sem("std3")
            rstd3 = sem("rstd3")
            h2_ready = sem("h2_ready")
            tr3 = sem("tr3")
            tr3_out = sem("tr3_out")
            g_ps = sem("g_ps")
            g_out = sem("g_out")
            out_ps = sem("out_ps")
            out_step = sem("out_step")
            out_ready = sem("out_ready")
            stored = [sem("stored0"), sem("stored1")]

            with nc.Block() as block:
                @block.sync
                def _(sp):
                    sp.dma_start(w1_in[:], w1.rearrange("(o p) i -> p o i", p=P)).then_inc(w1_loaded, 16)
                    for b in range(NBLK):
                        sp.wait_ge(out_ready, b + 1)
                        sp.dma_start(out[b * BN:(b + 1) * BN, :], result[b % 2][:]).then_inc(stored[b % 2], 16)
                    for k in range(2):
                        sp.wait_ge(stored[k], 16 * (NBLK // 2))

                @block.vector
                def _(dve):
                    for b in range(NBLK):
                        dve.bn_stats(stats[:, b, :], S[0:BN, b, :]).then_inc(stats_own, 1)
                    for b in range(NBLK):
                        dve.wait_ge(stats_own, b + 1)
                        dve.bn_aggr(mv[:, b, :], stats[:, b, :]).then_inc(var_ready, 1)
                    dve.wait_ge(std3, 1)
                    dve.reciprocal(rstd[0:BN, :], std[:]).then_inc(rstd3, 1)
                    dve.wait_ge(rstd3, 1)
                    dve.wait_ge(var_ready, NBLK)
                    dve.scalar_tensor_tensor(out=shift[0:BN, :], in0=mv[:, :, 0], scalar=-1.0, in1=rstd[0:BN, :],
                                             op0=ALU.mult, op1=ALU.mult).then_inc(rstd3, 1)
                    for b in range(NBLK):
                        o = psum[0:BN, 4 + b % 4, :]
                        res = result[b % 2]
                        dve.wait_ge(out_ps, b + 1)
                        if b >= 2:
                            dve.wait_ge(stored[b % 2], 16 * (b // 2))
                        if b >= 1:
                            dve.wait_ge(out_ready, b)
                        dve.tensor_scalar(neg_part[:], o, 0.0, alpha_t[0:BN, :], ALU.min, ALU.mult).then_inc(out_step, 1)
                        dve.wait_ge(out_step, 2 * b + 1)
                        dve.scalar_tensor_tensor(out=res[:], in0=o, scalar=0.0, in1=neg_part[:], op0=ALU.max,
                                                 op1=ALU.add).then_inc(out_step, 1)
                        dve.wait_ge(out_step, 2 * b + 2)
                        dve.tensor_tensor(res[:], res[:], S[0:BN, b, :], ALU.add).then_inc(out_ready, 1)

                @block.scalar
                def _(act):
                    act.wait_ge(var_ready, NBLK)
                    act.activation(std[:], mv[:, :, 1], ACT.Sqrt, bias=eps_t[0:BN, :]).then_inc(std3, 1)
                    for i in range(KC):
                        act.wait_ge(tr3, i + 1)
                        act.copy(w1T[:, i, :], psum[:, i % 2, :]).then_inc(tr3_out, 1)
                    act.wait_ge(rstd3, 2)
                    for b in range(NBLK):
                        if b >= 2:
                            act.wait_ge(tr3, KC + b - 1)
                        act.activation(h2[b % 2][:], S[0:BN, b, :], ACT.Relu, bias=shift[0:BN, b:b + 1],
                                       scale=rstd[0:BN, b:b + 1]).then_inc(h2_ready, 1)
                        if b >= 1:
                            act.wait_ge(g_ps, b)
                            act.copy(G[:, b - 1, :], psum[0:BN, 2 + (b - 1) % 2, :]).then_inc(g_out, 1)
                        act.wait_ge(tr3, KC + b + 1)
                        act.copy(h2T[b % 2][:], psum[:, b % 2, 0:KC * BN].rearrange("p (c n) -> p c n", c=KC)).then_inc(tr3_out, 1)
                    act.wait_ge(g_ps, NBLK)
                    act.copy(G[:, NBLK - 1, :], psum[0:BN, 2 + (NBLK - 1) % 2, :]).then_inc(g_out, 1)

                @block.tensor
                def _(pe):
                    pe.wait_ge(w1_loaded, 16)
                    for i in range(KC):
                        if i >= 2:
                            pe.wait_ge(tr3_out, i - 1)
                        for o in range(KC):
                            mm = pe.transpose(psum[:, i % 2, o * P:(o + 1) * P], w1_in[:, o, i * P:(i + 1) * P], ident[:])
                        mm.then_inc(tr3, 1)

                    def turn(b):
                        pe.wait_ge(h2_ready, b + 1)
                        pe.wait_ge(tr3_out, KC + b - 1)
                        for c in range(KC):
                            mm = pe.transpose(psum[:, b % 2, c * BN:(c + 1) * BN], h2[b % 2][:, c * P:(c + 1) * P],
                                              ident[0:BN, 0:BN])
                        mm.then_inc(tr3, 1)

                    turn(0)
                    for b in range(NBLK):
                        if b + 1 < NBLK:
                            turn(b + 1)
                        pe.wait_ge(tr3_out, KC + b + 1)
                        if b >= 2:
                            pe.wait_ge(g_out, b - 1)
                        for c in range(KC):
                            mm = pe.matmul(psum[0:BN, 2 + b % 2, :], h2T[b % 2][:, c, :], w1T[:, c, :],
                                           start=(c == 0), stop=(c == KC - 1))
                        mm.then_inc(g_ps, 1)
                    for d in range(NBLK):
                        if d >= 4:
                            pe.wait_ge(out_step, 2 * (d - 4) + 2)
                        for s in range(NBLK):
                            if d == 0:
                                pe.wait_ge(g_out, s + 1)
                            mm = pe.matmul(psum[0:BN, 4 + d % 4, :], M[:, s * NBLK + d, :], G[:, s, :],
                                           start=(s == 0), stop=(s == NBLK - 1))
                        mm.then_inc(out_ps, 1)
        scope.close()


_INS = ['x', 'src', 'dst', 'edge_weight', 'L0_gnn_W', 'L0_gnn_b', 'L1_gnn_W', 'L1_gnn_alpha']


def kernel(**inputs):
    import numpy as _np
    import concourse.bacc as _bacc
    from concourse import mybir as _mybir
    from concourse.bass_utils import run_bass_kernel_spmd as _run

    nc = _bacc.Bacc("TRN2", target_bir_lowering=False, num_devices=1)
    arrays, args = {}, []
    for name in _INS:
        a = _np.ascontiguousarray(inputs[name])
        arrays[f"in_{name}_dram"] = a
        args.append(nc.dram_tensor(f"in_{name}_dram", a.shape, _mybir.dt.from_np(a.dtype), kind="ExternalInput").ap())
    out = nc.dram_tensor("out_dram", (N, D), F32, kind="ExternalOutput").ap()
    build(nc, *args, out)
    r = _run(nc, [arrays], core_ids=[0])
    return r.results[0]["out_dram"]
```

```python
from contextlib import ExitStack

import concourse.bass as bass
from concourse import mybir

ALU = mybir.AluOpType
ACT = mybir.ActivationFunctionType
AX = mybir.AxisListType
F32 = mybir.dt.float32
F32R = mybir.dt.float32r
BF16 = mybir.dt.bfloat16
I32 = mybir.dt.int32

P = 128
N = 1250
D = 512
E = 41250
BN = 125
NBLK = N // BN
NBKT = NBLK * NBLK
EROWS = 125
ECOLS = E // EROWS
TILE = 128
GRP = 4
MAXT = (E + (TILE - 1) * NBKT) // TILE + NBLK * (GRP - 1)
NGRP = MAXT // GRP
NT = NGRP * GRP
FIELDS = 4
CCOL = 15
NCHUNK = ECOLS // CCOL
KC = D // P
OHW = BN + 1
MAGIC = 12582912.0
EPS = 1e-5
IN_RANGE = "the offsets come from counts of started blocks and buckets, 1 to 10 or 100 by construction"
assert EROWS * ECOLS == E and NCHUNK * CCOL == ECOLS and NCHUNK % 2 == 0 and NGRP % 2 == 0


def build(nc, x, src, dst, edge_weight, w0, b0, w1, alpha, out):
    table_dram = nc.dram_tensor("edge_table", [P * NT, FIELDS], F32).ap()
    with ExitStack() as top:
        def sb(name, shape, dt, scope=top, side="left"):
            return scope.enter_context(nc.sbuf_tensor(name, shape, dt, side=side))

        def sem(name):
            return top.enter_context(nc.semaphore(name))

        S = sb("S", [P, NBLK, D], F32)
        ident = sb("ident", [P, P], F32)
        iota = sb("iota", [P, NT], F32)
        table = sb("table", [P, NT, FIELDS], F32)
        expand_at = sb("expand_at", [1, NGRP, 2 * GRP], I32)
        gather_at = sb("gather_at", [1, NGRP, 2 * GRP], I32)
        ident_r = sb("ident_r", [P, P], F32R)
        ident_b = sb("ident_b", [P, P], BF16)
        alpha_t = sb("alpha_t", [P, 1], F32)
        eps_t = sb("eps_t", [P, 1], F32)
        neg_mean = sb("neg_mean", [P, NBLK], F32)
        rstd = sb("rstd", [P, NBLK], F32)
        shift = sb("shift", [P, NBLK], F32)

        scope_ab = ExitStack()
        a_hi = sb("a_hi", [BN, NBLK * D], F32R, scope_ab, "right")
        a_lo = sb("a_lo", [BN, NBLK * D], F32R, scope_ab, "right")
        b_hi = sb("b_hi", [BN, NBLK * D], F32R, scope_ab, "right")
        b_lo = sb("b_lo", [BN, NBLK * D], F32R, scope_ab, "right")

        with ExitStack() as scope:
            def sb1(name, shape, dt):
                return sb(name, shape, dt, scope)

            src_i = sb1("src_i", [EROWS, ECOLS], I32)
            dst_i = sb1("dst_i", [EROWS, ECOLS], I32)
            weight = sb1("weight", [EROWS, ECOLS], F32)
            node_f = sb1("node_f", [EROWS, 2, ECOLS], F32)
            blk_a = sb1("blk_a", [EROWS, 2, ECOLS], F32)
            blk_b = sb1("blk_b", [EROWS, 2, ECOLS], F32)
            weight_hi = sb1("weight_hi", [EROWS, ECOLS], F32R)
            bucket = sb1("bucket", [EROWS, ECOLS], F32)
            payload = sb1("payload", [EROWS, ECOLS, FIELDS], F32)
            onehot = [sb1(f"onehot{k}", [EROWS, CCOL, NBKT], BF16) for k in range(2)]
            minus_ident = sb1("minus_ident", [P, P], F32R)
            before = sb1("before", [P, P], F32)
            ones = sb1("ones", [P, P], F32)
            row_count = sb1("row_count", [EROWS, NBKT], F32)
            zt = sb1("zt", [EROWS, NBKT], F32)
            tiles_of = sb1("tiles_of", [EROWS, NBKT], F32)
            tiles_to = sb1("tiles_to", [EROWS, NBKT], F32)
            tile_base = sb1("tile_base", [EROWS, NBKT], F32)
            blk_small = sb1("blk_small", [EROWS, 6, NBLK], F32)
            ones_row = sb1("ones_row", [EROWS, NBKT], F32)
            slot_next = [sb1(f"slot_next{k}", [EROWS, NBKT], F32) for k in range(2)]
            picked = sb1("picked", [EROWS, NBKT], F32)
            slot = [sb1(f"slot{k}", [EROWS, CCOL], F32) for k in range(2)]
            slot_tile = sb1("slot_tile", [EROWS, 3, CCOL], F32)
            stage_row = [sb1(f"stage_row{k}", [EROWS, CCOL], I32) for k in range(2)]
            stage_pay = [sb1(f"stage_pay{k}", [EROWS, CCOL, FIELDS], F32) for k in range(2)]
            started = sb1("started", [NBKT, NT], F32)
            bkt_small = sb1("bkt_small", [NBKT, 8], F32)
            w_in = sb1("w_in", [P, KC, 2 * D], F32)
            w0T = sb1("w0T", [P, 2 * KC, D], F32)
            bias_row = sb1("bias_row", [1, D], F32)
            h1 = [sb1(f"h1_{k}", [BN, D], F32) for k in range(2)]
            h1T = [sb1(f"h1T{k}", [P, KC, BN], F32) for k in range(2)]
            gate = sb1("gate", [P, 2], F32)
            sums = sb1("sums", [BN, 3, NBLK], F32)

            psum = scope.enter_context(nc.psum_tensor("psum1", [P, 8, 512], F32))
            count_ps = psum[0:EROWS, 0, 0:NBKT]
            total_ps = psum[0:EROWS, 0, 128:128 + NBKT]
            above_ps = psum[0:EROWS, 0, 256:256 + NBKT]
            base_col_ps = psum[0:NBKT, 0, 384:385]

            edges_in = sem("edges_in")
            weight_in = sem("weight_in")
            x_in = sem("x_in")
            w_loaded = sem("w_loaded")
            small_in = sem("small_in")
            consts = sem("consts")
            dconst = sem("dconst")
            pool_own = sem("pool_own")
            cleared = sem("cleared")
            cleared_dram = sem("cleared_dram")
            vstep = sem("vstep")
            payload_done = sem("payload_done")
            hot_ready = sem("hot_ready")
            hot_used = sem("hot_used")
            counted = sem("counted")
            count_out = sem("count_out")
            totals = sem("totals")
            base_ready = sem("base_ready")
            base_col = sem("base_col")
            started_ready = sem("started_ready")
            tables_ps = sem("tables_ps")
            slots_moved = sem("slots_moved")
            slot_found = sem("slot_found")
            slot_math = sem("slot_math")
            staged = sem("staged")
            chunk_taken = sem("chunk_taken")
            scattered = [sem("scattered0"), sem("scattered1")]
            table_in = sem("table_in")
            act_own = sem("act_own")
            std_ready = sem("std_ready")
            rstd_ready = sem("rstd_ready")
            tr_ready = sem("tr_ready")
            tr_out = sem("tr_out")
            h_ready = sem("h_ready")
            hT_ready = sem("hT_ready")
            ab_ps = sem("ab_ps")
            ab_hi_out = sem("ab_hi_out")
            ab_low = sem("ab_low")
            ab_out = sem("ab_out")

            with nc.Block() as block:
                @block.sync
                def _(sp):
                    sp.dma_start(src_i[:], src.rearrange("(p c) -> p c", p=EROWS)).then_inc(edges_in, 16)
                    sp.dma_start(dst_i[:], dst.rearrange("(p c) -> p c", p=EROWS)).then_inc(edges_in, 16)
                    sp.dma_start(weight[:], edge_weight.rearrange("(p c) -> p c", p=EROWS)).then_inc(weight_in, 16)
                    sp.dma_start(S[0:BN], x.rearrange("(b p) d -> p b d", p=BN)).then_inc(x_in, 16)
                    sp.dma_start(w_in[:], w0.rearrange("(o p) i -> p o i", p=P)).then_inc(w_loaded, 16)
                    sp.dma_start(bias_row[:], b0.rearrange("(a d) -> a d", a=1)).then_inc(small_in, 16)
                    sp.dma_start(alpha_t[:], alpha.rearrange("(a d) -> a d", a=1).to_broadcast([P, 1])).then_inc(small_in, 16)
                    sp.wait_ge(cleared, 1)
                    sp.dma_start(table_dram.rearrange("(p t) f -> p (t f)", p=P),
                                 table.rearrange("p t f -> p (t f)")).then_inc(cleared_dram, 16)
                    for k in range(2):
                        sp.wait_ge(scattered[k], 16 * CCOL * (NCHUNK // 2))
                    sp.dma_start(table.rearrange("p t f -> p (t f)"),
                                 table_dram.rearrange("(p t) f -> p (t f)", p=P)).then_inc(table_in, 16)
                    sp.wait_ge(table_in, 16)
                    sp.wait_ge(small_in, 32)

                @block.gpsimd
                def _(pool):
                    pool.iota(iota[:], [[1, NT]], base=0, channel_multiplier=0,
                              allow_small_or_imprecise_dtypes=True).then_inc(consts, 1)
                    pool.memset(table[:], -1.0).then_inc(cleared, 1)
                    pool.memset(ones[:], 1.0).then_inc(pool_own, 1)
                    pool.wait_ge(pool_own, 1)
                    pool.affine_select(out=ident[:], in_=ones[:], compare_op=ALU.is_equal, fill=0.0, base=0,
                                       pattern=[[-1, P]], channel_multiplier=1).then_inc(consts, 1)
                    pool.affine_select(out=before[:], in_=ones[:], compare_op=ALU.is_gt, fill=0.0, base=0,
                                       pattern=[[1, P]], channel_multiplier=-1).then_inc(consts, 1)
                    pool.iota(bkt_small[:, 0:1], [[0, 1]], base=0, channel_multiplier=1,
                              allow_small_or_imprecise_dtypes=True).then_inc(consts, 1)
                    pool.wait_ge(cleared_dram, 16)
                    with pool.Fori(0, NCHUNK // 2) as it:
                        for k in range(2):
                            pool.wait_ge(staged, it * 4 + 2 * (k + 1))
                            pool.tensor_tensor(gate[:, k:k + 1], ones[:, 0:1], ones[:, 1:2],
                                               ALU.add).then_inc(chunk_taken, 1)
                            for c in range(CCOL):
                                pool.indirect_dma_start(
                                    table_dram[:, :], bass.IndirectOffsetOnAxis(ap=stage_row[k][:, c:c + 1], axis=0),
                                    stage_pay[k][:, c, :], None).then_inc(scattered[k], 16)

                @block.vector
                def _(dve):
                    steps = [0]

                    def own(ins):
                        steps[0] += 1
                        ins.then_inc(vstep, 1)
                        dve.wait_ge(vstep, steps[0])

                    dve.memset(eps_t[:], EPS).then_inc(dconst, 1)
                    dve.memset(ones_row[:], 1.0).then_inc(dconst, 1)
                    dve.wait_ge(edges_in, 32)
                    own(dve.tensor_copy(node_f[:, 0, :], src_i[:]))
                    own(dve.tensor_copy(node_f[:, 1, :], dst_i[:]))
                    own(dve.tensor_scalar(blk_a[:], node_f[:], -(BN - 1) / 2, 1.0 / BN, ALU.add, ALU.mult))
                    own(dve.tensor_scalar(blk_b[:], blk_a[:], MAGIC, None, ALU.add))
                    own(dve.tensor_scalar(blk_a[:], blk_b[:], -MAGIC, None, ALU.add))
                    own(dve.scalar_tensor_tensor(out=bucket[:], in0=blk_a[:, 0, :], scalar=float(NBLK),
                                                 in1=blk_a[:, 1, :], op0=ALU.mult, op1=ALU.add))
                    dve.wait_ge(consts, 1)
                    for c in range(NCHUNK):
                        if c >= 2:
                            dve.wait_ge(hot_used, c - 1)
                        dve.tensor_tensor(onehot[c % 2][:],
                                          bucket[:, c * CCOL:(c + 1) * CCOL].unsqueeze(2).to_broadcast([EROWS, CCOL, NBKT]),
                                          iota[0:EROWS, 0:NBKT].unsqueeze(1).to_broadcast([EROWS, CCOL, NBKT]),
                                          ALU.is_equal).then_inc(hot_ready, 1)
                    for k in range(2):
                        own(dve.scalar_tensor_tensor(out=payload[:, :, k], in0=blk_a[:, k, :], scalar=-float(BN),
                                                     in1=node_f[:, k, :], op0=ALU.mult, op1=ALU.add))
                    dve.wait_ge(weight_in, 16)
                    own(dve.tensor_copy(weight_hi[:], weight[:]))
                    own(dve.tensor_copy(payload[:, :, 2], weight_hi[:].bitcast(F32)))
                    own(dve.tensor_tensor(payload[:, :, 3], weight[:], weight_hi[:].bitcast(F32), ALU.subtract))
                    dve.wait_ge(counted, 1)
                    dve.tensor_copy(row_count[:], count_ps).then_inc(count_out, 1)
                    dve.wait_ge(totals, 1)
                    own(dve.tensor_scalar(zt[:], total_ps, (TILE - 1) / 2, 1.0 / TILE, ALU.add, ALU.mult))
                    own(dve.tensor_scalar(tiles_to[:], zt[:], MAGIC, None, ALU.add))
                    own(dve.tensor_scalar(tiles_of[:], tiles_to[:], -MAGIC, None, ALU.add))
                    in_blk, grp_a, grp_b, grp_to, start = (blk_small[:, k, :] for k in range(5))
                    own(dve.tensor_reduce(in_blk, tiles_of.rearrange("p (s d) -> p s d", s=NBLK), AX.X, ALU.add))
                    own(dve.tensor_scalar(grp_a, in_blk, (GRP - 1) / 2, 1.0 / GRP, ALU.add, ALU.mult))
                    own(dve.tensor_scalar(grp_b, grp_a, MAGIC, None, ALU.add))
                    own(dve.tensor_scalar(grp_a, grp_b, -MAGIC, None, ALU.add))
                    own(dve.tensor_tensor_scan(grp_to, ones_row[:, 0:NBLK], grp_a, 0.0, ALU.mult, ALU.add))
                    own(dve.tensor_tensor(grp_b, grp_to, grp_a, ALU.subtract))
                    own(dve.tensor_tensor_scan(tiles_to[:], ones_row[:], tiles_of[:], 0.0, ALU.mult, ALU.add))
                    own(dve.tensor_tensor(zt[:], tiles_to[:], tiles_of[:], ALU.subtract))
                    first_of_blk = zt.rearrange("p (s d) -> p s d", s=NBLK)[:, :, 0]
                    own(dve.scalar_tensor_tensor(out=start, in0=grp_b, scalar=float(GRP), in1=first_of_blk,
                                                 op0=ALU.mult, op1=ALU.subtract))
                    own(dve.tensor_tensor(tile_base.rearrange("p (s d) -> p s d", s=NBLK),
                                          zt.rearrange("p (s d) -> p s d", s=NBLK),
                                          start.unsqueeze(2).to_broadcast([EROWS, NBLK, NBLK]), ALU.add))
                    dve.scalar_tensor_tensor(out=slot_next[0][:], in0=tile_base[:], scalar=float(TILE), in1=above_ps,
                                             op0=ALU.mult, op1=ALU.add).then_inc(slots_moved, 1)
                    dve.memset(picked[:], 0.0).then_inc(slot_found, 1)
                    dve.wait_ge(std_ready, 1)
                    dve.reciprocal(rstd[0:BN, :], sums[:, 2, :]).then_inc(rstd_ready, 1)
                    dve.wait_ge(rstd_ready, 1)
                    dve.tensor_tensor(shift[0:BN, :], neg_mean[0:BN, :], rstd[0:BN, :], ALU.mult).then_inc(rstd_ready, 1)

                    def slots_of_chunk(it, k, first):
                        for c in range(CCOL):
                            n = it * (2 * CCOL) + (k * CCOL + c)
                            col = bucket[:, c + k * CCOL:c + k * CCOL + 1] if first else \
                                bucket[:, bass.ds(it * (2 * CCOL) + (k * CCOL + c), 1)]
                            now, then = slot_next[(k * CCOL + c) % 2], slot_next[(k * CCOL + c + 1) % 2]
                            dve.wait_ge(slots_moved, n + 1)
                            dve.wait_ge(slot_found, n + 1)
                            if c == 0 and not (first and k == 0):
                                dve.wait_ge(slot_math, (it * 2 + k) * 4)
                            dve.scalar_tensor_tensor(out=picked[:], in0=iota[0:EROWS, 0:NBKT], scalar=col, in1=now[:],
                                                     op0=ALU.is_equal, op1=ALU.mult,
                                                     accum_out=slot[k][:, c:c + 1]).then_inc(slot_found, 1)
                            dve.scalar_tensor_tensor(out=then[:], in0=iota[0:EROWS, 0:NBKT], scalar=col, in1=now[:],
                                                     op0=ALU.is_equal, op1=ALU.add).then_inc(slots_moved, 1)
                        base = (it * 2 + k) * 4
                        whole, tile_no, lane = (slot_tile[:, i, :] for i in range(3))
                        dve.wait_ge(slot_found, it * (2 * CCOL) + (k + 1) * CCOL + 1)
                        if not first:
                            dve.wait_ge(chunk_taken, it * 2 + (k - 1))
                            dve.wait_ge(scattered[k], it * (16 * CCOL))
                        if not (first and k == 0):
                            dve.wait_ge(staged, (it * 2 + k) * 2)
                        dve.tensor_scalar(whole, slot[k][:], -(TILE - 1) / 2, 1.0 / TILE, ALU.add, ALU.mult).then_inc(slot_math, 1)
                        dve.wait_ge(slot_math, base + 1)
                        dve.tensor_scalar(lane, whole, MAGIC, None, ALU.add).then_inc(slot_math, 1)
                        dve.wait_ge(slot_math, base + 2)
                        dve.tensor_scalar(tile_no, lane, -MAGIC, None, ALU.add).then_inc(slot_math, 1)
                        dve.wait_ge(slot_math, base + 3)
                        dve.scalar_tensor_tensor(out=lane, in0=tile_no, scalar=-float(TILE), in1=slot[k][:],
                                                 op0=ALU.mult, op1=ALU.add).then_inc(slot_math, 1)
                        dve.wait_ge(slot_math, base + 4)
                        dve.scalar_tensor_tensor(out=stage_row[k][:], in0=lane, scalar=float(NT), in1=tile_no,
                                                 op0=ALU.mult, op1=ALU.add).then_inc(staged, 1)
                        pay = payload[:, k * CCOL:(k + 1) * CCOL, :] if first else \
                            payload[:, bass.ds(it * (2 * CCOL) + k * CCOL, CCOL), :]
                        dve.tensor_copy(stage_pay[k][:], pay).then_inc(staged, 1)

                    slots_of_chunk(0, 0, True)
                    slots_of_chunk(0, 1, True)
                    with dve.Fori(1, NCHUNK // 2) as it:
                        slots_of_chunk(it, 0, False)
                        slots_of_chunk(it, 1, False)

                    dve.wait_ge(consts, 4)
                    dve.wait_ge(base_col, 1)
                    n_bkt, t1, t2, t3, src_start, col_base, dst_coef, all_one = (bkt_small[:, i:i + 1] for i in range(8))
                    own(dve.tensor_copy(col_base, base_col_ps))
                    own(dve.tensor_scalar(started[:], iota[0:NBKT, :], col_base, None, ALU.is_ge))
                    own(dve.tensor_scalar(t1, n_bkt, -(NBLK - 1) / 2, 1.0 / NBLK, ALU.add, ALU.mult))
                    own(dve.tensor_scalar(t2, t1, MAGIC, None, ALU.add))
                    own(dve.tensor_scalar(t3, t2, -MAGIC, -float(NBLK), ALU.add, ALU.mult))
                    own(dve.tensor_tensor(t1, n_bkt, t3, ALU.add))
                    own(dve.tensor_scalar(src_start, t1, 0.0, None, ALU.is_equal))
                    own(dve.tensor_scalar(dst_coef, src_start, -float(NBLK), 1.0, ALU.mult, ALU.add))
                    dve.memset(all_one, 1.0).then_inc(started_ready, 1)
                    dve.wait_ge(tables_ps, 1)
                    own(dve.tensor_scalar(expand_at[:, :, 0:GRP], psum[0:1, 1, 0:NT].rearrange("p (g j) -> p g j", j=GRP),
                                          float(NBLK - 1), float(D), ALU.add, ALU.mult))
                    own(dve.tensor_scalar(gather_at[:, :, 0:GRP], psum[0:1, 3, 0:NT].rearrange("p (g j) -> p g j", j=GRP),
                                          -1.0, float(BN), ALU.add, ALU.mult))
                    for at in (expand_at, gather_at):
                        own(dve.tensor_scalar(at[:, :, GRP], psum[0:1, 2, 0:NGRP], -1.0, float(D), ALU.add, ALU.mult))

                @block.tensor
                def _(pe):
                    pe.wait_ge(hot_ready, 1)
                    pe.wait_ge(ab_out, 1)
                    for c in range(NCHUNK):
                        pe.wait_ge(hot_ready, c + 1)
                        for k in range(CCOL):
                            mm = pe.matmul(count_ps, ident_b[0:EROWS, 0:EROWS], onehot[c % 2][:, k, :],
                                           start=(c == 0 and k == 0), stop=(c == NCHUNK - 1 and k == CCOL - 1))
                        mm.then_inc(counted if c == NCHUNK - 1 else hot_used, 1)
                    pe.wait_ge(count_out, 1)
                    pe.wait_ge(consts, 3)
                    pe.matmul(total_ps, ones[0:EROWS, 0:EROWS], row_count[:], start=True, stop=True)
                    pe.matmul(above_ps, before[0:EROWS, 0:EROWS], row_count[:], start=True, stop=True).then_inc(totals, 1)
                    pe.wait_ge(w_loaded, 16)
                    for i in range(2 * KC):
                        if i >= 2:
                            pe.wait_ge(tr_out, i - 1)
                        for o in range(KC):
                            mm = pe.transpose(psum[:, 4 + i % 2, o * P:(o + 1) * P], w_in[:, o, i * P:(i + 1) * P], ident[:])
                        mm.then_inc(tr_ready, 1)
                    pe.wait_ge(small_in, 32)
                    for b in range(NBLK):
                        pe.wait_ge(h_ready, b + 1)
                        pe.wait_ge(tr_out, 2 * KC + b - 1)
                        for c in range(KC):
                            mm = pe.transpose(psum[:, 4 + b % 2, c * BN:(c + 1) * BN], h1[b % 2][:, c * P:(c + 1) * P],
                                              ident[0:BN, 0:BN])
                        mm.then_inc(tr_ready, 1)
                        pe.wait_ge(tr_out, 2 * KC + b + 1)
                        for m in range(2):
                            if b >= 1:
                                pe.wait_ge(ab_out, 2 * b + m)
                            ps = psum[0:BN, 6 + m, :]
                            if m == 0:
                                pe.matmul(ps, ones[0:1, 0:BN], bias_row[:], start=True, stop=False)
                            for c in range(KC):
                                mm = pe.matmul(ps, h1T[b % 2][:, c, :], w0T[:, m * KC + c, :],
                                               start=(m == 1 and c == 0), stop=(c == KC - 1))
                            mm.then_inc(ab_ps, 1)
                        for m in range(2):
                            pe.wait_ge(ab_hi_out, 2 * b + m + 1)
                            pe.matmul(psum[0:BN, 6 + m, :], minus_ident[0:BN, 0:BN],
                                      (a_hi, b_hi)[m][:, b * D:(b + 1) * D], start=False, stop=True,
                                      skip_group_check=True).then_inc(ab_low, 1)
                    pe.wait_ge(slots_moved, 1)
                    pe.matmul(base_col_ps, tile_base[0:1, :], ones[0:1, 0:1], start=True, stop=True).then_inc(base_col, 1)
                    pe.wait_ge(started_ready, 1)
                    pe.matmul(psum[0:1, 1, 0:NT], bkt_small[:, 6:7], started[:], start=True, stop=True)
                    pe.matmul(psum[0:1, 2, 0:NGRP], bkt_small[:, 4:5], started[:, 0:NT:GRP], start=True, stop=True)
                    pe.matmul(psum[0:1, 3, 0:NT], bkt_small[:, 7:8], started[:], start=True, stop=True).then_inc(tables_ps, 1)

                @block.scalar
                def _(act):
                    act.wait_ge(consts, 3)
                    act.copy(ident_b[:], ident[:]).then_inc(ab_out, 1)
                    act.mul(minus_ident[:], ident[:], -1.0).then_inc(act_own, 1)
                    act.copy(ident_r[:], ident[:]).then_inc(act_own, 1)
                    act.wait_ge(x_in, 16)
                    steps = 2
                    for b in range(NBLK):
                        act.wait_ge(act_own, steps)
                        act.activation(h1[0][:], S[0:BN, b, :], ACT.Identity, accum_out=sums[:, 0, b:b + 1]).then_inc(act_own, 1)
                        steps += 1
                    act.wait_ge(act_own, steps)
                    act.mul(neg_mean[0:BN, :], sums[:, 0, :], -1.0 / D).then_inc(act_own, 1)
                    steps += 1
                    for b in range(NBLK):
                        act.wait_ge(act_own, steps)
                        act.activation(h1[0][:], S[0:BN, b, :], ACT.Square, bias=neg_mean[0:BN, b:b + 1],
                                       accum_out=sums[:, 1, b:b + 1]).then_inc(act_own, 1)
                        steps += 1
                    act.wait_ge(act_own, steps)
                    act.wait_ge(dconst, 2)
                    act.activation(sums[:, 2, :], sums[:, 1, :], ACT.Sqrt, bias=eps_t[0:BN, :],
                                   scale=1.0 / D).then_inc(std_ready, 1)
                    for i in range(2 * KC):
                        act.wait_ge(tr_ready, i + 1)
                        act.copy(w0T[:, i, :], psum[:, 4 + i % 2, :]).then_inc(tr_out, 1)
                    act.wait_ge(rstd_ready, 2)

                    def normed(b):
                        if b >= 2:
                            act.wait_ge(tr_ready, 2 * KC + b - 1)
                        act.activation(h1[b % 2][:], S[0:BN, b, :], ACT.Relu, bias=shift[0:BN, b:b + 1],
                                       scale=rstd[0:BN, b:b + 1]).then_inc(h_ready, 1)

                    normed(0)
                    for b in range(NBLK):
                        act.wait_ge(tr_ready, 2 * KC + b + 1)
                        if b >= 2:
                            act.wait_ge(ab_ps, 2 * b - 2)
                        act.copy(h1T[b % 2][:], psum[:, 4 + b % 2, 0:KC * BN].rearrange("p (c n) -> p c n", c=KC)).then_inc(tr_out, 1)
                        if b + 1 < NBLK:
                            normed(b + 1)
                        for m in range(2):
                            act.wait_ge(ab_ps, 2 * b + m + 1)
                            act.copy((a_hi, b_hi)[m][:, b * D:(b + 1) * D], psum[0:BN, 6 + m, :]).then_inc(ab_hi_out, 1)
                        for m in range(2):
                            act.wait_ge(ab_low, 2 * b + m + 1)
                            act.copy((a_lo, b_lo)[m][:, b * D:(b + 1) * D], psum[0:BN, 6 + m, :]).then_inc(ab_out, 1)

        scope = ExitStack()
        M = sb("M", [BN, NBKT, BN], F32, scope)
        hot_s = [sb(f"hot_s{k}", [P, GRP, OHW], F32R, scope) for k in range(2)]
        hot_d = [sb(f"hot_d{k}", [P, GRP, OHW], BF16, scope) for k in range(2)]
        hot_w = sb("hot_w", [P, 2, GRP, OHW], F32R, scope)
        turned_s = [sb(f"turned_s{k}", [BN, GRP * P], F32R, scope) for k in range(2)]
        turned_d = [sb(f"turned_d{k}", [BN, GRP * P], F32R, scope) for k in range(2)]
        msg_hi = [sb(f"msg_hi{k}", [P, D], F32R, scope) for k in range(GRP)]
        msg_lo = [sb(f"msg_lo{k}", [P, D], F32R, scope) for k in range(GRP)]

        psum_scope = ExitStack()
        edge_ps = [psum_scope.enter_context(nc.psum_tensor(f"edge_ps{k}", [P, D], F32)) for k in range(GRP)]
        turn_ps = psum_scope.enter_context(nc.psum_tensor("turn_ps", [BN, GRP * P], F32))
        node_ps = [psum_scope.enter_context(nc.psum_tensor(f"node_ps{k}", [BN, D], F32)) for k in range(2)]
        m_ps = psum_scope.enter_context(nc.psum_tensor("m_ps", [BN, GRP, P], F32))

        m_clear = sem("m_clear")
        hots_s = sem("hots_s")
        hots_d = sem("hots_d")
        hots_w = sem("hots_w")
        turn_ready = sem("turn_ready")
        turned = sem("turned")
        edge_ready = sem("edge_ready")
        hi_ready = sem("hi_ready")
        lo_ready = sem("lo_ready")
        tile_summed = sem("tile_summed")
        m_ready = sem("m_ready")
        node_added = sem("node_added")
        m_added = sem("m_added")

        with nc.Block() as block:
            @block.gpsimd
            def _(pool):
                def group(g, k, first=False):
                    rows = table[:, bass.ds(g * GRP, GRP), :]
                    pool.wait_ge(hots_d, g + 1)
                    if not first:
                        pool.wait_ge(m_ready, g)
                    for f in range(2):
                        pool.tensor_tensor(hot_w[:, f], hot_d[k][:],
                                           rows[:, :, 2 + f:3 + f].to_broadcast([P, GRP, OHW]),
                                           ALU.mult).then_inc(hots_w, 1)

                group(0, 0, first=True)
                group(1, 1)
                with pool.Fori(1, NGRP // 2) as it:
                    group(it * 2, 0)
                    group(it * 2 + 1, 1)

            @block.tensor
            def _(pe):
                def turn(hot, identity):
                    for j in range(GRP):
                        mm = pe.matmul(turn_ps[:, j * P:(j + 1) * P], hot[:, j, 0:BN], identity[:],
                                       start=True, stop=True)
                    mm.then_inc(turn_ready, 1)

                def sum_tile(g, j, k):
                    pe.wait_ge(lo_ready, g * GRP + j + 1)
                    pe.matmul(node_ps[k][:], hot_s[k][:, j, 0:BN], msg_hi[j][:], start=(j == 0), stop=False)
                    pe.matmul(node_ps[k][:], hot_s[k][:, j, 0:BN], msg_lo[j][:], start=False,
                              stop=(j == GRP - 1)).then_inc(tile_summed, 1)

                def weights(g, k):
                    pe.wait_ge(hots_w, g * 2 + 2)
                    for j in range(GRP):
                        for f in range(2):
                            mm = pe.matmul(m_ps[:, j, 0:OHW], hot_s[k][:, j, 0:BN], hot_w[:, f, j, :],
                                           start=(f == 0), stop=(f == 1))
                    mm.then_inc(m_ready, 1)

                def offsets(g):
                    _, at = nc.values_load_multi_w_load_instructions(
                        expand_at[0:1, bass.ds(g, 1), 0:GRP + 1].rearrange("p g j -> p (g j)"),
                        engines=[mybir.EngineType.PE], min_val=0, max_val=(NBLK - 1) * D,
                        skip_runtime_bounds_check_because=IN_RANGE)
                    return at

                def group(g, k, at, first=False, last=False):
                    a_rows = bass.ds(at[GRP], D)
                    for j in range(GRP):
                        b_rows = bass.ds(at[j], D)
                        ts, td = turned_s[k][:, j * P:(j + 1) * P], turned_d[k][:, j * P:(j + 1) * P]
                        if j == 0:
                            pe.wait_ge(turned, g * 2 + 1)
                        pe.matmul(edge_ps[j][:], td, b_hi[:, b_rows], start=True, stop=False)
                        pe.matmul(edge_ps[j][:], td, b_lo[:, b_rows], start=False, stop=False)
                        if j == 0:
                            pe.wait_ge(turned, g * 2 + 2)
                        pe.matmul(edge_ps[j][:], ts, a_hi[:, a_rows], start=False, stop=False)
                        pe.matmul(edge_ps[j][:], ts, a_lo[:, a_rows], start=False, stop=True).then_inc(edge_ready, 1)
                        if j == 3 and not last:
                            pe.wait_ge(hots_s, g + 2)
                            pe.wait_ge(turned, g * 2 + 3)
                            turn(hot_s[1 - k], ident_r)
                        if j >= 2:
                            sum_tile(g, j - 2, k)
                        elif not first:
                            sum_tile(g - 1, j + 2, 1 - k)
                        if j == 1 and not first:
                            weights(g - 1, 1 - k)
                        if j == 2 and not last:
                            pe.wait_ge(hots_d, g + 2)
                            turn(hot_d[1 - k], ident_b)

                pe.wait_ge(hots_d, 1)
                turn(hot_d[0], ident_b)
                pe.wait_ge(hots_s, 1)
                pe.wait_ge(turned, 1)
                turn(hot_s[0], ident_r)
                group(0, 0, offsets(0), first=True)
                group(1, 1, offsets(1))
                with pe.Fori(1, NGRP // 2 - 1) as it:
                    at0, at1 = offsets(it * 2), offsets(it * 2 + 1)
                    group(it * 2, 0, at0)
                    group(it * 2 + 1, 1, at1)
                group(NGRP - 2, 0, offsets(NGRP - 2))
                group(NGRP - 1, 1, offsets(NGRP - 1), last=True)
                sum_tile(NGRP - 1, 2, 1)
                sum_tile(NGRP - 1, 3, 1)
                weights(NGRP - 1, 1)

            @block.scalar
            def _(act):
                def group(g, k, first=False, last=False):
                    for j in range(GRP):
                        act.wait_ge(edge_ready, g * GRP + j + 1)
                        act.activation(msg_hi[j][:], edge_ps[j][:], ACT.Relu).then_inc(hi_ready, 1)
                        if j == 2 and not last:
                            act.wait_ge(turn_ready, g * 2 + 3)
                            act.copy(turned_d[1 - k][:], turn_ps[:]).then_inc(turned, 1)
                        if j == 3 and not last:
                            act.wait_ge(turn_ready, g * 2 + 4)
                            act.copy(turned_s[1 - k][:], turn_ps[:]).then_inc(turned, 1)

                act.wait_ge(turn_ready, 1)
                act.copy(turned_d[0][:], turn_ps[:]).then_inc(turned, 1)
                act.wait_ge(turn_ready, 2)
                act.copy(turned_s[0][:], turn_ps[:]).then_inc(turned, 1)
                group(0, 0, first=True)
                group(1, 1)
                with act.Fori(1, NGRP // 2 - 1) as it:
                    group(it * 2, 0)
                    group(it * 2 + 1, 1)
                group(NGRP - 2, 0)
                group(NGRP - 1, 1, last=True)

            @block.vector
            def _(dve):
                def offsets(g):
                    _, at = nc.values_load_multi_w_load_instructions(
                        gather_at[0:1, bass.ds(g, 1), 0:GRP + 1].rearrange("p g j -> p (g j)"),
                        engines=[mybir.EngineType.DVE], min_val=0, max_val=(NBKT - 1) * BN,
                        skip_runtime_bounds_check_because=IN_RANGE)
                    return at

                def add_sums(g, k, at, first=False):
                    dve.wait_ge(tile_summed, g * GRP + GRP)
                    if not first:
                        dve.wait_ge(node_added, g)
                    row = nc.s_assert_within(at[GRP], 0, (NBLK - 1) * D, skip_runtime_bounds_check_because=IN_RANGE)
                    rows = S.rearrange("p b d -> p (b d)")[0:BN, bass.ds(row, D)]
                    dve.tensor_tensor(rows, rows, node_ps[k][:], ALU.add).then_inc(node_added, 1)

                def add_weights(g, at, first=False):
                    flat = M.rearrange("p b n -> p (b n)")
                    dve.wait_ge(m_ready, g + 1)
                    for j in range(GRP):
                        if not (first and j == 0):
                            dve.wait_ge(m_added, g * GRP + j)
                        part = flat[:, bass.ds(at[j], BN)]
                        dve.tensor_tensor(part, part, m_ps[:, j, 0:BN], ALU.add).then_inc(m_added, 1)

                def make_hots(hot, field, g, ready):
                    local = table[:, bass.ds(g * GRP, GRP), field:field + 1]
                    dve.tensor_tensor(hot[:], iota[:, 0:OHW].unsqueeze(1).to_broadcast([P, GRP, OHW]),
                                      local.to_broadcast([P, GRP, OHW]), ALU.is_equal).then_inc(ready, 1)

                def group(g, k, before, first=False, second=False, last=False):
                    for j in range(GRP):
                        dve.wait_ge(hi_ready, g * GRP + j + 1)
                        dve.scalar_tensor_tensor(out=msg_lo[j][:], in0=edge_ps[j][:], scalar=0.0,
                                                 in1=msg_hi[j][:].bitcast(F32), op0=ALU.max,
                                                 op1=ALU.subtract).then_inc(lo_ready, 1)
                        if j == 0 and not last:
                            if not first:
                                dve.wait_ge(hots_w, g * 2)
                            make_hots(hot_d[1 - k], 1, g + 1, hots_d)
                        if j == 1:
                            if not last:
                                if not first:
                                    dve.wait_ge(m_ready, g)
                                make_hots(hot_s[1 - k], 0, g + 1, hots_s)
                            if not first:
                                add_sums(g - 1, 1 - k, before, first=second)
                        if j == 2 and not first:
                            add_weights(g - 1, before, first=second)

                make_hots(hot_d[0], 1, 0, hots_d)
                make_hots(hot_s[0], 0, 0, hots_s)
                dve.memset(M[:], 0.0).then_inc(m_clear, 1)
                dve.wait_ge(m_clear, 1)
                group(0, 0, None, first=True)
                group(1, 1, offsets(0), second=True)
                with dve.Fori(1, NGRP // 2 - 1) as it:
                    at0, at1 = offsets(it * 2 - 1), offsets(it * 2)
                    group(it * 2, 0, at0)
                    group(it * 2 + 1, 1, at1)
                group(NGRP - 2, 0, offsets(NGRP - 3))
                group(NGRP - 1, 1, offsets(NGRP - 2), last=True)
                at = offsets(NGRP - 1)
                add_weights(NGRP - 1, at)
                add_sums(NGRP - 1, 1, at)

        psum_scope.close()
        scope_ab.close()
        with ExitStack() as tail:
            def sb3(name, shape, dt):
                return sb(name, shape, dt, tail, "right")

            G = sb3("G", [BN, NBLK, D], F32)
            w1_in = sb3("w1_in", [P, KC, D], F32)
            w1T = sb3("w1T", [P, KC, D], F32)
            h2 = [sb3(f"h2_{k}", [BN, D], F32) for k in range(2)]
            h2T = [sb3(f"h2T{k}", [P, KC, BN], F32) for k in range(2)]
            result = [sb3(f"result{k}", [BN, D], F32) for k in range(2)]
            neg_part = sb3("neg_part", [BN, D], F32)
            stats = sb3("stats", [BN, NBLK, nc.vector.BN_STATS_DIM], F32)
            mv = sb3("mv", [BN, NBLK, nc.vector.BN_AGGR_DIM], F32)
            std = sb3("std", [BN, NBLK], F32)
            psum = tail.enter_context(nc.psum_tensor("psum3", [P, 8, 512], F32))
            w1_loaded = sem("w1_loaded")
            stats_own = sem("stats_own")
            var_ready = sem("var_ready")
            std3 = sem("std3")
            rstd3 = sem("rstd3")
            h2_ready = sem("h2_ready")
            tr3 = sem("tr3")
            tr3_out = sem("tr3_out")
            g_ps = sem("g_ps")
            g_out = sem("g_out")
            out_ps = sem("out_ps")
            out_step = sem("out_step")
            out_ready = sem("out_ready")
            stored = [sem("stored0"), sem("stored1")]

            with nc.Block() as block:
                @block.sync
                def _(sp):
                    sp.dma_start(w1_in[:], w1.rearrange("(o p) i -> p o i", p=P)).then_inc(w1_loaded, 16)
                    for b in range(NBLK):
                        sp.wait_ge(out_ready, b + 1)
                        sp.dma_start(out[b * BN:(b + 1) * BN, :], result[b % 2][:]).then_inc(stored[b % 2], 16)
                    for k in range(2):
                        sp.wait_ge(stored[k], 16 * (NBLK // 2))

                @block.vector
                def _(dve):
                    for b in range(NBLK):
                        dve.bn_stats(stats[:, b, :], S[0:BN, b, :]).then_inc(stats_own, 1)
                    for b in range(NBLK):
                        dve.wait_ge(stats_own, b + 1)
                        dve.bn_aggr(mv[:, b, :], stats[:, b, :]).then_inc(var_ready, 1)
                    dve.wait_ge(std3, 1)
                    dve.reciprocal(rstd[0:BN, :], std[:]).then_inc(rstd3, 1)
                    dve.wait_ge(rstd3, 1)
                    dve.wait_ge(var_ready, NBLK)
                    dve.scalar_tensor_tensor(out=shift[0:BN, :], in0=mv[:, :, 0], scalar=-1.0, in1=rstd[0:BN, :],
                                             op0=ALU.mult, op1=ALU.mult).then_inc(rstd3, 1)
                    for b in range(NBLK):
                        o = psum[0:BN, 4 + b % 4, :]
                        res = result[b % 2]
                        dve.wait_ge(out_ps, b + 1)
                        if b >= 2:
                            dve.wait_ge(stored[b % 2], 16 * (b // 2))
                        if b >= 1:
                            dve.wait_ge(out_ready, b)
                        dve.tensor_scalar(neg_part[:], o, 0.0, alpha_t[0:BN, :], ALU.min, ALU.mult).then_inc(out_step, 1)
                        dve.wait_ge(out_step, 2 * b + 1)
                        dve.scalar_tensor_tensor(out=res[:], in0=o, scalar=0.0, in1=neg_part[:], op0=ALU.max,
                                                 op1=ALU.add).then_inc(out_step, 1)
                        dve.wait_ge(out_step, 2 * b + 2)
                        dve.tensor_tensor(res[:], res[:], S[0:BN, b, :], ALU.add).then_inc(out_ready, 1)

                @block.scalar
                def _(act):
                    act.wait_ge(var_ready, NBLK)
                    act.activation(std[:], mv[:, :, 1], ACT.Sqrt, bias=eps_t[0:BN, :]).then_inc(std3, 1)
                    for i in range(KC):
                        act.wait_ge(tr3, i + 1)
                        act.copy(w1T[:, i, :], psum[:, i % 2, :]).then_inc(tr3_out, 1)
                    act.wait_ge(rstd3, 2)
                    for b in range(NBLK):
                        if b >= 2:
                            act.wait_ge(tr3, KC + b - 1)
                        act.activation(h2[b % 2][:], S[0:BN, b, :], ACT.Relu, bias=shift[0:BN, b:b + 1],
                                       scale=rstd[0:BN, b:b + 1]).then_inc(h2_ready, 1)
                        if b >= 1:
                            act.wait_ge(g_ps, b)
                            act.copy(G[:, b - 1, :], psum[0:BN, 2 + (b - 1) % 2, :]).then_inc(g_out, 1)
                        act.wait_ge(tr3, KC + b + 1)
                        act.copy(h2T[b % 2][:], psum[:, b % 2, 0:KC * BN].rearrange("p (c n) -> p c n", c=KC)).then_inc(tr3_out, 1)
                    act.wait_ge(g_ps, NBLK)
                    act.copy(G[:, NBLK - 1, :], psum[0:BN, 2 + (NBLK - 1) % 2, :]).then_inc(g_out, 1)

                @block.tensor
                def _(pe):
                    pe.wait_ge(w1_loaded, 16)
                    for i in range(KC):
                        if i >= 2:
                            pe.wait_ge(tr3_out, i - 1)
                        for o in range(KC):
                            mm = pe.transpose(psum[:, i % 2, o * P:(o + 1) * P], w1_in[:, o, i * P:(i + 1) * P], ident[:])
                        mm.then_inc(tr3, 1)

                    def turn(b):
                        pe.wait_ge(h2_ready, b + 1)
                        pe.wait_ge(tr3_out, KC + b - 1)
                        for c in range(KC):
                            mm = pe.transpose(psum[:, b % 2, c * BN:(c + 1) * BN], h2[b % 2][:, c * P:(c + 1) * P],
                                              ident[0:BN, 0:BN])
                        mm.then_inc(tr3, 1)

                    turn(0)
                    for b in range(NBLK):
                        if b + 1 < NBLK:
                            turn(b + 1)
                        pe.wait_ge(tr3_out, KC + b + 1)
                        if b >= 2:
                            pe.wait_ge(g_out, b - 1)
                        for c in range(KC):
                            mm = pe.matmul(psum[0:BN, 2 + b % 2, :], h2T[b % 2][:, c, :], w1T[:, c, :],
                                           start=(c == 0), stop=(c == KC - 1))
                        mm.then_inc(g_ps, 1)
                    for d in range(NBLK):
                        if d >= 4:
                            pe.wait_ge(out_step, 2 * (d - 4) + 2)
                        for s in range(NBLK):
                            if d == 0:
                                pe.wait_ge(g_out, s + 1)
                            mm = pe.matmul(psum[0:BN, 4 + d % 4, :], M[:, s * NBLK + d, :], G[:, s, :],
                                           start=(s == 0), stop=(s == NBLK - 1))
                        mm.then_inc(out_ps, 1)
        scope.close()


_INS = ['x', 'src', 'dst', 'edge_weight', 'L0_gnn_W', 'L0_gnn_b', 'L1_gnn_W', 'L1_gnn_alpha']


def kernel(**inputs):
    import numpy as _np
    import concourse.bacc as _bacc
    from concourse import mybir as _mybir
    from concourse.bass_utils import run_bass_kernel_spmd as _run

    nc = _bacc.Bacc("TRN2", target_bir_lowering=False, num_devices=1)
    arrays, args = {}, []
    for name in _INS:
        a = _np.ascontiguousarray(inputs[name])
        arrays[f"in_{name}_dram"] = a
        args.append(nc.dram_tensor(f"in_{name}_dram", a.shape, _mybir.dt.from_np(a.dtype), kind="ExternalInput").ap())
    out = nc.dram_tensor("out_dram", (N, D), F32, kind="ExternalOutput").ap()
    build(nc, *args, out)
    r = _run(nc, [arrays], core_ids=[0])
    return r.results[0]["out_dram"]
```

```python
from contextlib import ExitStack

import concourse.bass as bass
from concourse import mybir

ALU = mybir.AluOpType
ACT = mybir.ActivationFunctionType
AX = mybir.AxisListType
F32 = mybir.dt.float32
F32R = mybir.dt.float32r
BF16 = mybir.dt.bfloat16
F16 = mybir.dt.float16
I32 = mybir.dt.int32

P = 128
N = 1250
D = 512
E = 41250
BN = 125
NBLK = N // BN
NBKT = NBLK * NBLK
EROWS = 125
ECOLS = E // EROWS
TILE = 128
GRP = 4
PAIR = 2
MAXT = (E + (TILE - 1) * NBKT) // TILE + NBLK * (PAIR - 1)
NGRP = -(-MAXT // GRP)
NT = NGRP * GRP
FIELDS = 2
COUNT_COLS = 15
NCOUNT = ECOLS // COUNT_COLS
ACT_COUNT = 8
DVE_COUNT = NCOUNT - ACT_COUNT
CCOL = 15
DMA_COLS = 10
PE_COLS = CCOL - DMA_COLS
COLS_BETWEEN = (range(0, 2), range(2, 4), range(4, 6), range(6, 8), range(8, 10))
COLS_BETWEEN_LAST = (range(0, 1), range(1, 3), range(3, 5), range(5, 7), range(7, 10))
PIECES = 5
RING = 5
NEXT = 3
NCHUNK = ECOLS // CCOL
UNROLL = 4
KC = D // P
OHW = BN + 1
MAGIC = 12582912.0
EPS = 1e-5
IN_RANGE = "the offsets come from counts of started blocks and buckets, 1 to 10 or 100 by construction"
assert EROWS * ECOLS == E and NCOUNT * COUNT_COLS == ECOLS and NCHUNK * CCOL == ECOLS
assert NCHUNK == 2 * (NBLK + 1), "a block of A and B goes with two chunks of edges, the first two have none"
assert (NGRP - 4) % UNROLL == 0 and UNROLL % 2 == 0


def build(nc, x, src, dst, edge_weight, w0, b0, w1, alpha, out):
    table_dram = nc.dram_tensor("edge_table", [P * NT, FIELDS], F32).ap()
    with ExitStack() as top:
        def sb(name, shape, dt, scope=top, side="left"):
            return scope.enter_context(nc.sbuf_tensor(name, shape, dt, side=side))

        def sem(name):
            return top.enter_context(nc.semaphore(name))

        S = sb("S", [P, NBLK, D], F32)
        ident = sb("ident", [P, P], F32)
        iota = sb("iota", [P, NT], F32)
        local_s = sb("local_s", [P, NT], F32)
        local_d = sb("local_d", [P, NT], F32)
        weight_h = sb("weight_h", [P, NT], F32R)
        weight_l = sb("weight_l", [P, NT], F32)
        expand_at = sb("expand_at", [1, NGRP, 2 * GRP], I32)
        gather_at = sb("gather_at", [1, NGRP, 2 * GRP], I32)
        ident_b = sb("ident_b", [P, P], BF16)
        alpha_t = sb("alpha_t", [P, 1], F32)
        minus_no = sb("minus_no", [P, 1], F32)
        eps_t = sb("eps_t", [P, 1], F32)
        neg_mean = sb("neg_mean", [P, NBLK], F32)
        rstd = sb("rstd", [P, NBLK], F32)
        shift = sb("shift", [P, NBLK], F32)

        scope_ab = ExitStack()
        a_hi = sb("a_hi", [BN, NBLK * D], F32R, scope_ab, "right")
        a_lo = sb("a_lo", [BN, NBLK * D], F32R, scope_ab, "right")
        b_hi = sb("b_hi", [BN, NBLK * D], F32R, scope_ab, "right")
        b_lo = sb("b_lo", [BN, NBLK * D], F32R, scope_ab, "right")

        with ExitStack() as scope:
            def sb1(name, shape, dt):
                return sb(name, shape, dt, scope)

            src_i = sb1("src_i", [EROWS, ECOLS], I32)
            dst_i = sb1("dst_i", [EROWS, ECOLS], I32)
            weight = sb1("weight", [EROWS, ECOLS], F32)
            node_f = sb1("node_f", [EROWS, 2, ECOLS], F32)
            blk_a = sb1("blk_a", [EROWS, 2, ECOLS], F32)
            blk_b = sb1("blk_b", [EROWS, 2, ECOLS], F32)
            bucket = sb1("bucket", [EROWS, ECOLS], F32)
            payload = sb1("payload", [EROWS, ECOLS, FIELDS], F32)
            pieces = sb1("pieces", [EROWS, ECOLS, PIECES], BF16)
            raw = sb1("raw", [P, NT, FIELDS], F32)
            code, weight_all = raw[:, :, 0], raw[:, :, 1]
            iota_h = sb1("iota_h", [EROWS, NT], F16)
            hot_tile = [sb1(f"hot_tile{k}", [EROWS, NT], BF16) for k in range(RING)]
            hot_lane = [sb1(f"hot_lane{k}", [EROWS, TILE], BF16) for k in range(RING)]
            lane_piece_all = sb1("lane_piece", [EROWS, RING * PIECES * TILE], BF16)
            lane_piece = [lane_piece_all[:, k * PIECES * TILE:(k + 1) * PIECES * TILE]
                          .rearrange("p (q l) -> p q l", q=PIECES) for k in range(RING)]
            onehot = [sb1(f"onehot{k}", [EROWS, COUNT_COLS, NBKT], BF16) for k in range(2)]
            onehot_act = [lane_piece_all[:, k * COUNT_COLS * NBKT:(k + 1) * COUNT_COLS * NBKT]
                          .rearrange("p (c b) -> p c b", c=COUNT_COLS) for k in range(2)]
            minus_ident = sb1("minus_ident", [P, P], F32R)
            before = sb1("before", [P, P], F32)
            ones = sb1("ones", [P, P], F32)
            row_count = sb1("row_count", [EROWS, NBKT], F32)
            zt = sb1("zt", [EROWS, NBKT], F32)
            tiles_of = sb1("tiles_of", [EROWS, NBKT], F32)
            tiles_to = sb1("tiles_to", [EROWS, NBKT], F32)
            tile_base = sb1("tile_base", [EROWS, NBKT], F32)
            blk_small = sb1("blk_small", [EROWS, 6, NBLK], F32)
            ones_row = sb1("ones_row", [EROWS, NBKT], F32)
            slot_next = [sb1(f"slot_next{k}", [EROWS, NBKT], F32) for k in range(NEXT)]
            picked = [sb1(f"picked{k}", [EROWS, NBKT], F32) for k in range(2)]
            slot = [sb1(f"slot{k}", [EROWS, CCOL], F32) for k in range(2)]
            tile_no = [sb1(f"tile_no{k}", [EROWS, CCOL], F32) for k in range(2)]
            lane = [sb1(f"lane{k}", [EROWS, CCOL], F32) for k in range(2)]
            slot_tmp = sb1("slot_tmp", [EROWS, 2, CCOL], F32)
            stage_row = [sb1(f"stage_row{k}", [EROWS, DMA_COLS], I32) for k in range(2)]
            stage_pay = [sb1(f"stage_pay{k}", [EROWS, DMA_COLS, FIELDS], F32) for k in range(2)]
            stage_piece = [sb1(f"stage_piece{k}", [EROWS, PE_COLS, PIECES], F32) for k in range(2)]
            started = sb1("started", [NBKT, NT], F32)
            bkt_small = sb1("bkt_small", [NBKT, 8], F32)
            w_in = sb1("w_in", [P, KC, 2 * D], F32)
            w0T = sb1("w0T", [P, 2 * KC, D], F32)
            apart = [w0T.rearrange("p c d -> p (c d)")[0:EROWS, k * 3 * D:k * 3 * D + COUNT_COLS * NBKT]
                     .rearrange("p (c b) -> p c b", c=COUNT_COLS) for k in range(2)]
            bias_row = sb1("bias_row", [1, D], F32)
            n_bkt, t1, t2, t3, src_start, col_base, dst_coef, all_one = (bkt_small[:, i:i + 1] for i in range(8))
            h1 = sb1("h1", [BN, D], F32)
            h1T = sb1("h1T", [P, KC, BN], F32)
            gate = sb1("gate", [P, 2], F32)
            sums = sb1("sums", [BN, 3, NBLK], F32)

            psum = scope.enter_context(nc.psum_tensor("psum1", [P, 8, 512], F32))
            count_ps = psum[0:EROWS, 0, 0:NBKT]
            total_ps = psum[0:EROWS, 0, 128:128 + NBKT]
            above_ps = psum[0:EROWS, 0, 256:256 + NBKT]
            base_col_ps = psum[0:NBKT, 0, 384:385]
            code_ps = psum[:, 2, 0:NT]
            weight_ps = psum[:, 3, 0:NT]

            edges_in = sem("edges_in")
            weight_in = sem("weight_in")
            x_in = sem("x_in")
            w_loaded = sem("w_loaded")
            small_in = sem("small_in")
            consts = sem("consts")
            dconst = sem("dconst")
            pool_own = sem("pool_own")
            cleared = sem("cleared")
            cleared_dram = sem("cleared_dram")
            vstep = sem("vstep")
            payload_done = sem("payload_done")
            hot_ready = sem("hot_ready")
            hot_used = sem("hot_used")
            bucket_ready = sem("bucket_ready")
            apart_ready = sem("apart_ready")
            apart_square = sem("apart_square")
            hot_act_ready = sem("hot_act_ready")
            hot_act_used = sem("hot_act_used")
            counted = sem("counted")
            count_out = sem("count_out")
            totals = sem("totals")
            base_col = sem("base_col")
            base_out = sem("base_out")
            table_coef = sem("table_coef")
            weights_ready = sem("weights_ready")
            started_ready = sem("started_ready")
            tables_ps = sem("tables_ps")
            tables_out = sem("tables_out")
            slot_step = sem("slot_step")
            col_hot = sem("col_hot")
            pieces_ready = sem("pieces_ready")
            placed = sem("placed")
            slot_math = sem("slot_math")
            staged = sem("staged")
            chunk_taken = sem("chunk_taken")
            scattered = [sem("scattered0"), sem("scattered1")]
            table_in = sem("table_in")
            act_own = sem("act_own")
            std_ready = sem("std_ready")
            rstd_ready = sem("rstd_ready")
            tr_ready = sem("tr_ready")
            tr_out = sem("tr_out")
            h_ready = sem("h_ready")
            ab_ps = sem("ab_ps")
            ab_hi_out = sem("ab_hi_out")
            ab_low = sem("ab_low")
            ab_out = sem("ab_out")

            with nc.Block() as block:
                @block.sync
                def _(sp):
                    sp.dma_start(src_i[:], src.rearrange("(p c) -> p c", p=EROWS)).then_inc(edges_in, 16)
                    sp.dma_start(dst_i[:], dst.rearrange("(p c) -> p c", p=EROWS)).then_inc(edges_in, 16)
                    sp.dma_start(weight[:], edge_weight.rearrange("(p c) -> p c", p=EROWS)).then_inc(weight_in, 16)
                    sp.dma_start(S[0:BN], x.rearrange("(b p) d -> p b d", p=BN)).then_inc(x_in, 16)
                    sp.dma_start(w_in[:], w0.rearrange("(o p) i -> p o i", p=P)).then_inc(w_loaded, 16)
                    sp.dma_start(bias_row[:], b0.rearrange("(a d) -> a d", a=1)).then_inc(small_in, 16)
                    sp.dma_start(alpha_t[:], alpha.rearrange("(a d) -> a d", a=1).to_broadcast([P, 1])).then_inc(small_in, 16)
                    sp.wait_ge(cleared, 1)
                    sp.dma_start(table_dram.rearrange("(p t) f -> p (t f)", p=P),
                                 raw.rearrange("p t f -> p (t f)")).then_inc(cleared_dram, 16)
                    for k in range(2):
                        sp.wait_ge(scattered[k], 16 * DMA_COLS * (NCHUNK // 2))
                    sp.dma_start(raw.rearrange("p t f -> p (t f)"),
                                 table_dram.rearrange("(p t) f -> p (t f)", p=P)).then_inc(table_in, 16)
                    sp.wait_ge(table_in, 16)
                    sp.wait_ge(small_in, 32)

                @block.gpsimd
                def _(pool):
                    pool.iota(iota[:], [[1, NT]], base=0, channel_multiplier=0,
                              allow_small_or_imprecise_dtypes=True).then_inc(consts, 1)
                    pool.memset(raw[:], 0.0).then_inc(cleared, 1)
                    pool.memset(ones[:], 1.0).then_inc(pool_own, 1)
                    pool.wait_ge(pool_own, 1)
                    pool.affine_select(out=ident[:], in_=ones[:], compare_op=ALU.is_equal, fill=0.0, base=0,
                                       pattern=[[-1, P]], channel_multiplier=1).then_inc(consts, 1)
                    pool.affine_select(out=before[:], in_=ones[:], compare_op=ALU.is_gt, fill=0.0, base=0,
                                       pattern=[[1, P]], channel_multiplier=-1).then_inc(consts, 1)
                    pool.iota(bkt_small[:, 0:1], [[0, 1]], base=0, channel_multiplier=1,
                              allow_small_or_imprecise_dtypes=True).then_inc(consts, 1)
                    pool.iota(minus_no[:], [[0, 1]], base=-1, channel_multiplier=-1,
                              allow_small_or_imprecise_dtypes=True).then_inc(consts, 1)
                    pool.wait_ge(bucket_ready, 1)
                    for c in range(ACT_COUNT):
                        if c >= 2:
                            pool.wait_ge(hot_act_ready, c - 1)
                        shape = [EROWS, COUNT_COLS, NBKT]
                        n = (DVE_COUNT + c) * COUNT_COLS
                        pool.tensor_tensor(apart[c % 2], bucket[:, n:n + COUNT_COLS].unsqueeze(2).to_broadcast(shape),
                                           iota[0:EROWS, 0:NBKT].unsqueeze(1).to_broadcast(shape),
                                           ALU.subtract).then_inc(apart_ready, 1)
                    steps = [1]

                    def own(ins):
                        steps[0] += 1
                        ins.then_inc(pool_own, 1)
                        pool.wait_ge(pool_own, steps[0])

                    own(pool.tensor_scalar(blk_b[:], blk_a[:], -float(BN), 1.0, ALU.mult, ALU.add))
                    own(pool.tensor_tensor(blk_b[:], blk_b[:], node_f[:], ALU.add))
                    own(pool.tensor_copy(pieces[:, :, 0], blk_b[:, 0, :]))
                    own(pool.tensor_scalar(pieces[:, :, 1], blk_b[:, 1, :], float(TILE), None, ALU.mult))
                    own(pool.tensor_tensor(payload[:, :, 0], pieces[:, :, 0], pieces[:, :, 1], ALU.add))
                    pool.wait_ge(weight_in, 16)
                    own(pool.tensor_copy(payload[:, :, 1], weight[:]))
                    left = weight[:]
                    for k in range(2, PIECES):
                        own(pool.tensor_copy(pieces[:, :, k], left))
                        if k < PIECES - 1:
                            own(pool.tensor_tensor(blk_b[:, k % 2, :], left, pieces[:, :, k], ALU.subtract))
                            left = blk_b[:, k % 2, :]
                    pool.memset(all_one, 1.0).then_inc(payload_done, 1)
                    own(pool.tensor_scalar(t1, n_bkt, -(NBLK - 1) / 2, 1.0 / NBLK, ALU.add, ALU.mult))
                    own(pool.tensor_scalar(t2, t1, MAGIC, None, ALU.add))
                    own(pool.tensor_scalar(t3, t2, -MAGIC, -float(NBLK), ALU.add, ALU.mult))
                    own(pool.tensor_tensor(t1, n_bkt, t3, ALU.add))
                    own(pool.tensor_scalar(t2, t1, -1.0, 1.0, ALU.mult, ALU.add))
                    own(pool.tensor_scalar(src_start, t2, 0.0, None, ALU.max))
                    pool.tensor_scalar(dst_coef, src_start, -float(NBLK), 1.0, ALU.mult, ALU.add).then_inc(table_coef, 1)
                    pool.wait_ge(cleared_dram, 16)
                    with pool.Fori(0, NCHUNK // 2) as it:
                        for k in range(2):
                            pool.wait_ge(staged, it * 4 + 2 * (k + 1))
                            pool.tensor_tensor(gate[:, k:k + 1], ones[:, 0:1], ones[:, 1:2],
                                               ALU.add).then_inc(chunk_taken, 1)
                            for c in range(DMA_COLS):
                                pool.indirect_dma_start(
                                    table_dram[:, :], bass.IndirectOffsetOnAxis(ap=stage_row[k][:, c:c + 1], axis=0),
                                    stage_pay[k][:, c, :], None).then_inc(scattered[k], 16)

                    pool.wait_ge(weights_ready, 1)
                    own(pool.tensor_copy(weight_h[:], weight_all))
                    pool.tensor_tensor(weight_l[:], weight_all, weight_h[:].bitcast(F32), ALU.subtract)

                @block.vector
                def _(dve):
                    steps = [0]

                    def own(ins):
                        steps[0] += 1
                        ins.then_inc(vstep, 1)
                        dve.wait_ge(vstep, steps[0])

                    dve.memset(eps_t[:], EPS).then_inc(dconst, 1)
                    dve.memset(ones_row[:], 1.0).then_inc(dconst, 1)
                    dve.wait_ge(edges_in, 32)
                    own(dve.tensor_copy(node_f[:, 0, :], src_i[:]))
                    own(dve.tensor_copy(node_f[:, 1, :], dst_i[:]))
                    own(dve.tensor_scalar(blk_a[:], node_f[:], -(BN - 1) / 2, 1.0 / BN, ALU.add, ALU.mult))
                    own(dve.tensor_scalar(blk_b[:], blk_a[:], MAGIC, None, ALU.add))
                    own(dve.tensor_scalar(blk_a[:], blk_b[:], -MAGIC, None, ALU.add))
                    dve.scalar_tensor_tensor(out=bucket[:], in0=blk_a[:, 0, :], scalar=float(NBLK),
                                             in1=blk_a[:, 1, :], op0=ALU.mult, op1=ALU.add).then_inc(bucket_ready, 1)
                    dve.wait_ge(bucket_ready, 1)
                    dve.wait_ge(consts, 1)
                    for c in range(DVE_COUNT):
                        if c >= 2:
                            dve.wait_ge(hot_used, c - 1)
                        shape = [EROWS, COUNT_COLS, NBKT]
                        dve.tensor_tensor(onehot[c % 2][:],
                                          bucket[:, c * COUNT_COLS:(c + 1) * COUNT_COLS].unsqueeze(2).to_broadcast(shape),
                                          iota[0:EROWS, 0:NBKT].unsqueeze(1).to_broadcast(shape), ALU.is_equal).then_inc(hot_ready, 1)
                    own(dve.tensor_copy(iota_h[:], iota[0:EROWS, :]))
                    dve.wait_ge(counted, 2)
                    dve.tensor_copy(row_count[:], count_ps).then_inc(count_out, 1)
                    dve.wait_ge(totals, 1)
                    own(dve.tensor_scalar(zt[:], total_ps, (TILE - 1) / 2, 1.0 / TILE, ALU.add, ALU.mult))
                    own(dve.tensor_scalar(tiles_to[:], zt[:], MAGIC, None, ALU.add))
                    own(dve.tensor_scalar(tiles_of[:], tiles_to[:], -MAGIC, None, ALU.add))
                    in_blk, pair_a, pair_b, pair_to, start = (blk_small[:, k, :] for k in range(5))
                    own(dve.tensor_reduce(in_blk, tiles_of.rearrange("p (s d) -> p s d", s=NBLK), AX.X, ALU.add))
                    own(dve.tensor_scalar(pair_a, in_blk, (PAIR - 1) / 2, 1.0 / PAIR, ALU.add, ALU.mult))
                    own(dve.tensor_scalar(pair_b, pair_a, MAGIC, None, ALU.add))
                    own(dve.tensor_scalar(pair_a, pair_b, -MAGIC, None, ALU.add))
                    own(dve.tensor_tensor_scan(pair_to, ones_row[:, 0:NBLK], pair_a, 0.0, ALU.mult, ALU.add))
                    own(dve.tensor_tensor(pair_b, pair_to, pair_a, ALU.subtract))
                    own(dve.tensor_tensor_scan(tiles_to[:], ones_row[:], tiles_of[:], 0.0, ALU.mult, ALU.add))
                    own(dve.tensor_tensor(zt[:], tiles_to[:], tiles_of[:], ALU.subtract))
                    first_of_blk = zt.rearrange("p (s d) -> p s d", s=NBLK)[:, :, 0]
                    own(dve.scalar_tensor_tensor(out=start, in0=pair_b, scalar=float(PAIR), in1=first_of_blk,
                                                 op0=ALU.mult, op1=ALU.subtract))
                    own(dve.tensor_tensor(tile_base.rearrange("p (s d) -> p s d", s=NBLK),
                                          zt.rearrange("p (s d) -> p s d", s=NBLK),
                                          start.unsqueeze(2).to_broadcast([EROWS, NBLK, NBLK]), ALU.add))
                    dve.scalar_tensor_tensor(out=slot_next[0][:], in0=tile_base[:], scalar=float(TILE), in1=above_ps,
                                             op0=ALU.mult, op1=ALU.add).then_inc(slot_step, 1)

                    def hot_column(m, k, i, first):
                        r = (k * PE_COLS + i) % RING
                        if not first:
                            dve.wait_ge(placed, m * PE_COLS + (i + 1 - RING))
                        c = DMA_COLS + i
                        dve.tensor_scalar(hot_tile[r][:], iota_h[:], tile_no[k][:, c:c + 1], None, ALU.is_equal)
                        dve.tensor_scalar(hot_lane[r][:], iota_h[:, 0:TILE], lane[k][:, c:c + 1], None,
                                          ALU.is_equal).then_inc(col_hot, 1)

                    def slots_of_chunk(it, k, first=False, behind=True):
                        m = it * 2 + k
                        for c in range(CCOL):
                            n = it * (2 * CCOL) + (k * CCOL + c)
                            col = bucket[:, c + k * CCOL:c + k * CCOL + 1] if first else bucket[:, bass.ds(n, 1)]
                            now, then = slot_next[c % NEXT], slot_next[(c + 1) % NEXT]
                            dve.wait_ge(slot_step, 1 if first and k + c == 0 else n * 2)
                            dve.scalar_tensor_tensor(out=then[:], in0=iota[0:EROWS, 0:NBKT], scalar=col, in1=now[:],
                                                     op0=ALU.is_equal, op1=ALU.add).then_inc(slot_step, 1)
                            dve.scalar_tensor_tensor(out=picked[(k * CCOL + c) % 2][:], in0=iota[0:EROWS, 0:NBKT],
                                                     scalar=col, in1=now[:], op0=ALU.is_equal, op1=ALU.mult,
                                                     accum_out=slot[k][:, c:c + 1]).then_inc(slot_step, 1)
                            if behind and c % 3 == 2:
                                if c == 2:
                                    dve.wait_ge(slot_math, m * 4)
                                hot_column(m - 1, 1 - k, c // 3, first)
                        whole, shifted = slot_tmp[:, 0, :], slot_tmp[:, 1, :]
                        dve.wait_ge(slot_step, it * (4 * CCOL) + (2 * (k + 1) * CCOL + 1))
                        if not first:
                            dve.wait_ge(chunk_taken, m - 1)
                            dve.wait_ge(scattered[k], it * (16 * DMA_COLS))
                            dve.wait_ge(pieces_ready, m * PE_COLS - PE_COLS)
                        if not (first and k == 0):
                            dve.wait_ge(staged, m * 2)
                        dve.tensor_scalar(whole, slot[k][:], -(TILE - 1) / 2, 1.0 / TILE, ALU.add, ALU.mult).then_inc(slot_math, 1)
                        dve.wait_ge(slot_math, m * 4 + 1)
                        dve.tensor_scalar(shifted, whole, MAGIC, None, ALU.add).then_inc(slot_math, 1)
                        dve.wait_ge(slot_math, m * 4 + 2)
                        dve.tensor_scalar(tile_no[k][:], shifted, -MAGIC, None, ALU.add).then_inc(slot_math, 1)
                        dve.wait_ge(slot_math, m * 4 + 3)
                        dve.scalar_tensor_tensor(out=lane[k][:], in0=tile_no[k][:], scalar=-float(TILE), in1=slot[k][:],
                                                 op0=ALU.mult, op1=ALU.add).then_inc(slot_math, 1)
                        if first and k == 0:
                            dve.wait_ge(payload_done, 1)
                        cols = payload[:, k * CCOL:k * CCOL + DMA_COLS, :] if first else \
                            payload[:, bass.ds(m * CCOL, DMA_COLS), :]
                        dve.tensor_copy(stage_pay[k][:], cols).then_inc(staged, 1)
                        dve.wait_ge(slot_math, m * 4 + 4)
                        dve.scalar_tensor_tensor(out=stage_row[k][:], in0=lane[k][:, 0:DMA_COLS], scalar=float(NT),
                                                 in1=tile_no[k][:, 0:DMA_COLS], op0=ALU.mult, op1=ALU.add).then_inc(staged, 1)
                        cols = pieces[:, k * CCOL + DMA_COLS:(k + 1) * CCOL, :] if first else \
                            pieces[:, bass.ds(m * CCOL + DMA_COLS, PE_COLS), :]
                        dve.tensor_copy(stage_piece[k][:], cols)

                    slots_of_chunk(0, 0, first=True, behind=False)
                    dve.wait_ge(base_col, 1)
                    dve.tensor_copy(col_base, base_col_ps).then_inc(base_out, 1)
                    dve.wait_ge(base_out, 1)
                    dve.tensor_scalar(started[:], iota[0:NBKT, :], col_base, None, ALU.is_ge).then_inc(started_ready, 1)
                    dve.wait_ge(std_ready, 1)
                    dve.reciprocal(rstd[0:BN, :], sums[:, 2, :]).then_inc(rstd_ready, 1)
                    dve.wait_ge(rstd_ready, 1)
                    dve.tensor_tensor(shift[0:BN, :], neg_mean[0:BN, :], rstd[0:BN, :], ALU.mult).then_inc(rstd_ready, 1)
                    slots_of_chunk(0, 1, first=True)
                    with dve.Fori(1, NCHUNK // 2) as it:
                        slots_of_chunk(it, 0)
                        slots_of_chunk(it, 1)
                    dve.wait_ge(slot_math, NCHUNK * 4)
                    for i in range(PE_COLS):
                        hot_column(NCHUNK - 1, 1, i, False)

                    dve.wait_ge(placed, NCHUNK * PE_COLS)
                    dve.wait_ge(table_in, 16)
                    dve.tensor_tensor(weight_all, weight_all, weight_ps, ALU.add).then_inc(weights_ready, 1)
                    own(dve.tensor_tensor(code, code, code_ps, ALU.add))
                    own(dve.tensor_scalar(local_s[:], code, -(TILE - 2) / 2, 1.0 / TILE, ALU.add, ALU.mult))
                    own(dve.tensor_scalar(local_d[:], local_s[:], MAGIC, None, ALU.add))
                    own(dve.tensor_scalar(local_d[:], local_d[:], -MAGIC, None, ALU.add))
                    own(dve.scalar_tensor_tensor(out=local_s[:], in0=local_d[:], scalar=-float(TILE), in1=code,
                                                 op0=ALU.mult, op1=ALU.add))

                @block.tensor
                def _(pe):
                    pe.wait_ge(ab_out, 1)
                    order = sorted([(c + 0.5, 0, c) for c in range(DVE_COUNT)] +
                                   [((c + 1) * DVE_COUNT / ACT_COUNT, 1, c) for c in range(ACT_COUNT)])
                    for n, (_, by_act, c) in enumerate(order):
                        pe.wait_ge(hot_act_ready if by_act else hot_ready, c + 1)
                        for k in range(COUNT_COLS):
                            mm = pe.matmul(count_ps, ident_b[0:EROWS, 0:EROWS],
                                           (onehot_act if by_act else onehot)[c % 2][:, k, :],
                                           start=(n == 0 and k == 0), stop=(n == NCOUNT - 1 and k == COUNT_COLS - 1))
                        mm.then_inc(counted if n >= NCOUNT - 2 else hot_act_used if by_act else hot_used, 1)
                    pe.wait_ge(count_out, 1)
                    pe.wait_ge(consts, 3)
                    pe.matmul(total_ps, ones[0:EROWS, 0:EROWS], row_count[:], start=True, stop=True)
                    pe.matmul(above_ps, before[0:EROWS, 0:EROWS], row_count[:], start=True, stop=True).then_inc(totals, 1)
                    pe.wait_ge(w_loaded, 16)
                    for i in range(2 * KC):
                        if i == 2:
                            pe.wait_ge(slot_step, 1)
                            pe.matmul(base_col_ps, tile_base[0:1, :], ones[0:1, 0:1],
                                      start=True, stop=True).then_inc(base_col, 1)
                        if i >= 2:
                            pe.wait_ge(tr_out, i - 1)
                        for o in range(KC):
                            mm = pe.transpose(psum[:, 4 + i % 2, o * P:(o + 1) * P], w_in[:, o, i * P:(i + 1) * P], ident[:])
                        mm.then_inc(tr_ready, 1)
                    pe.wait_ge(started_ready, 1)
                    pe.wait_ge(table_coef, 1)
                    pe.wait_ge(tr_out, 2 * KC)
                    pe.matmul(psum[0:1, 1, 0:NT], dst_coef, started[:], start=True, stop=True)
                    pe.matmul(psum[0:1, 4, 0:NT // PAIR], src_start, started[:, 0:NT:PAIR], start=True, stop=True)
                    pe.matmul(psum[0:1, 5, 0:NT], all_one, started[:], start=True, stop=True).then_inc(tables_ps, 1)
                    pe.wait_ge(small_in, 32)

                    def place(it, cols, first=False):
                        for i in cols:
                            pe.wait_ge(pieces_ready, it * (2 * PE_COLS) + i + 1)
                            for q in range(PIECES):
                                mm = pe.matmul(code_ps if q < 2 else weight_ps, lane_piece[i % RING][:, q, :],
                                               hot_tile[i % RING][:], start=(first and i == 0 and q in (0, 2)),
                                               stop=True, skip_group_check=True)
                            mm.then_inc(placed, 1)

                    def product(b, m):
                        pe.wait_ge(ab_out, b * 2 + 1)
                        ps = psum[0:BN, 6 + m, :]
                        if m == 0:
                            pe.matmul(ps, ones[0:1, 0:BN], bias_row[:], start=True, stop=False)
                        for c in range(KC):
                            mm = pe.matmul(ps, h1T[:, c, :], w0T[:, m * KC + c, :],
                                           start=(m == 1 and c == 0), stop=(c == KC - 1))
                        mm.then_inc(ab_ps, 1)

                    def step(it, cols=COLS_BETWEEN):
                        b = it - 1
                        pe.wait_ge(tr_out, b + 2 * KC)
                        pe.wait_ge(h_ready, b + 1)
                        for c in range(KC):
                            mm = pe.transpose(psum[:, 4, c * BN:(c + 1) * BN], h1[:, c * P:(c + 1) * P], ident[0:BN, 0:BN])
                        mm.then_inc(tr_ready, 1)
                        place(it, cols[0])
                        pe.wait_ge(tr_out, b + 2 * KC + 1)
                        product(b, 0)
                        place(it, cols[1])
                        product(b, 1)
                        place(it, cols[2])
                        for m in range(2):
                            pe.wait_ge(ab_hi_out, b * 2 + m + 1)
                            pe.matmul(psum[0:BN, 6 + m, :], minus_ident[0:BN, 0:BN],
                                      (a_hi, b_hi)[m][:, bass.ds(b * D, D)], start=False, stop=True,
                                      skip_group_check=True).then_inc(ab_low, 1)
                        place(it, cols[3])
                        place(it, cols[4])

                    place(0, range(2 * PE_COLS), first=True)
                    pe.wait_ge(tables_out, 1)
                    with pe.Fori(1, NBLK) as it:
                        step(it)
                    step(NBLK, COLS_BETWEEN_LAST)

                @block.scalar
                def _(act):
                    act.wait_ge(consts, 3)
                    act.copy(ident_b[:], ident[:]).then_inc(ab_out, 1)
                    act.mul(minus_ident[:], ident[:], -1.0).then_inc(act_own, 1)
                    for c in range(ACT_COUNT):
                        act.wait_ge(apart_ready, c + 1)
                        act.activation(apart[c % 2], apart[c % 2], ACT.Square).then_inc(apart_square, 1)
                        if c >= 2:
                            act.wait_ge(hot_act_used, c - 1)
                        act.wait_ge(apart_square, c + 1)
                        act.activation(onehot_act[c % 2], apart[c % 2], ACT.Relu, bias=1.0,
                                       scale=-1.0).then_inc(hot_act_ready, 1)
                    act.wait_ge(x_in, 16)
                    steps = 1
                    for b in range(NBLK):
                        act.wait_ge(act_own, steps)
                        act.activation(h1[:], S[0:BN, b, :], ACT.Identity, accum_out=sums[:, 0, b:b + 1]).then_inc(act_own, 1)
                        steps += 1
                    act.wait_ge(act_own, steps)
                    act.mul(neg_mean[0:BN, :], sums[:, 0, :], -1.0 / D).then_inc(act_own, 1)
                    steps += 1
                    for b in range(NBLK):
                        act.wait_ge(act_own, steps)
                        act.activation(h1[:], S[0:BN, b, :], ACT.Square, bias=neg_mean[0:BN, b:b + 1],
                                       accum_out=sums[:, 1, b:b + 1]).then_inc(act_own, 1)
                        steps += 1
                    act.wait_ge(act_own, steps)
                    act.wait_ge(dconst, 2)
                    act.activation(sums[:, 2, :], sums[:, 1, :], ACT.Sqrt, bias=eps_t[0:BN, :],
                                   scale=1.0 / D).then_inc(std_ready, 1)
                    for i in range(2 * KC):
                        act.wait_ge(tr_ready, i + 1)
                        act.copy(w0T[:, i, :], psum[:, 4 + i % 2, :]).then_inc(tr_out, 1)
                    def pieces_of(it, cols):
                        for i in cols:
                            act.wait_ge(col_hot, it * (2 * PE_COLS) + i + 1)
                            for q in range(PIECES):
                                ins = act.activation(lane_piece[i % RING][:, q, :], hot_lane[i % RING][:], ACT.Copy,
                                                     scale=stage_piece[i // PE_COLS][:, i % PE_COLS, q:q + 1])
                            ins.then_inc(pieces_ready, 1)

                    def out_of_psum(b, m, part, done):
                        cols = bass.ds(b * D, D)
                        act.copy((a_hi, b_hi, a_lo, b_lo)[2 * part + m][:, cols], psum[0:BN, 6 + m, :]).then_inc(done, 1)

                    def step(it, cols=COLS_BETWEEN):
                        b = it - 1
                        act.wait_ge(tr_ready, b + 2 * KC)
                        act.activation(h1[:], S.rearrange("p b d -> p (b d)")[0:BN, bass.ds(b * D, D)], ACT.Relu,
                                       bias=shift[0:BN, bass.ds(b, 1)], scale=rstd[0:BN, bass.ds(b, 1)]).then_inc(h_ready, 1)
                        pieces_of(it, cols[0])
                        act.wait_ge(tr_ready, b + 2 * KC + 1)
                        act.copy(h1T[:], psum[:, 4, 0:KC * BN].rearrange("p (c n) -> p c n", c=KC)).then_inc(tr_out, 1)
                        pieces_of(it, cols[1])
                        act.wait_ge(ab_ps, b * 2 + 1)
                        out_of_psum(b, 0, 0, ab_hi_out)
                        pieces_of(it, cols[2])
                        act.wait_ge(ab_ps, b * 2 + 2)
                        out_of_psum(b, 1, 0, ab_hi_out)
                        pieces_of(it, cols[3])
                        for m in range(2):
                            act.wait_ge(ab_low, b * 2 + m + 1)
                            out_of_psum(b, m, 1, ab_out)
                        pieces_of(it, cols[4])

                    pieces_of(0, range(2 * PE_COLS))
                    act.wait_ge(tables_ps, 1)
                    act.activation(expand_at[:, :, 0:GRP], psum[0:1, 1, 0:NT].rearrange("p (g j) -> p g j", j=GRP),
                                   ACT.Copy, bias=float((NBLK - 1) * D), scale=float(D))
                    act.activation(gather_at[:, :, 0:GRP], psum[0:1, 5, 0:NT].rearrange("p (g j) -> p g j", j=GRP),
                                   ACT.Copy, bias=-float(BN), scale=float(BN))
                    for at in (expand_at, gather_at):
                        ins = act.activation(at[:, :, GRP:GRP + 2],
                                             psum[0:1, 4, 0:NT // PAIR].rearrange("p (g h) -> p g h", h=2),
                                             ACT.Copy, bias=-float(D), scale=float(D))
                    ins.then_inc(tables_out, 1)
                    act.wait_ge(rstd_ready, 2)
                    with act.Fori(1, NBLK) as it:
                        step(it)
                    step(NBLK, COLS_BETWEEN_LAST)

        scope_m, scope = ExitStack(), ExitStack()
        M = sb("M", [BN, NBKT, BN], F32, scope_m)
        hot_s = [sb(f"hot_s{k}", [P, GRP, OHW], F32R, scope) for k in range(2)]
        hot_d = [sb(f"hot_d{k}", [P, GRP, OHW], BF16, scope) for k in range(2)]
        hot_w = [sb(f"hot_w{h}", [P, PAIR, 2, OHW], F32R, scope) for h in range(2)]
        pair_w = [sb(f"pair_w{h}", [BN, PAIR, 2, OHW], F32, scope) for h in range(2)]
        row_s = sb("row_s", [NGRP, GRP * P], BF16, scope)
        row_d = sb("row_d", [NGRP, GRP * P], BF16, scope)
        square = sb("square", [BN, GRP * P], F32, scope)
        turned_s = [sb(f"turned_s{k}", [BN, GRP * P], F32R, scope) for k in range(2)]
        turned_d = [sb(f"turned_d{k}", [BN, GRP * P], F32R, scope) for k in range(2)]
        msg_hi = [sb(f"msg_hi{k}", [P, D], F32R, scope) for k in range(GRP)]
        msg_lo = [sb(f"msg_lo{k}", [P, D], F32R, scope) for k in range(GRP)]

        psum_scope = ExitStack()
        edge_ps = [psum_scope.enter_context(nc.psum_tensor(f"edge_ps{k}", [P, D], F32)) for k in range(GRP)]
        spread_ps = psum_scope.enter_context(nc.psum_tensor("spread_ps", [BN, GRP * P], F32))
        node_ps = [psum_scope.enter_context(nc.psum_tensor(f"node_ps{k}", [BN, D], F32)) for k in range(2)]
        m_ps = psum_scope.enter_context(nc.psum_tensor("m_ps", [BN, PAIR, 2, OHW], F32))

        m_clear = sem("m_clear")
        hots_d = sem("hots_d")
        rows_ps = sem("rows_ps")
        rows_out = sem("rows_out")
        hots_w = sem("hots_w")
        spread_ready = sem("spread_ready")
        squared = sem("squared")
        turned = sem("turned")
        edge_ready = sem("edge_ready")
        hi_ready = sem("hi_ready")
        lo_ready = sem("lo_ready")
        tile_summed = sem("tile_summed")
        m_ready = sem("m_ready")
        m_copied = sem("m_copied")
        node_added = sem("node_added")
        m_joined = sem("m_joined")
        m_added = sem("m_added")

        with nc.Block() as block:
            @block.gpsimd
            def _(pool):
                def offsets(g, h):
                    _, at = nc.values_load_multi_w_load_instructions(
                        gather_at[0:1, bass.ds(g, 1), h * PAIR:(h + 1) * PAIR].rearrange("p g j -> p (g j)"),
                        engines=[mybir.EngineType.Pool], min_val=0, max_val=(NBKT - 1) * BN,
                        skip_runtime_bounds_check_because=IN_RANGE)
                    return at

                def weigh(g, k, h, first=False):
                    if h == 0:
                        pool.wait_ge(hots_d, g + 1)
                    if not first:
                        pool.wait_ge(m_ready, g * 2 + h - 1)
                    for f, part in enumerate((weight_h[:].bitcast(F32), weight_l)):
                        pool.tensor_tensor(hot_w[h][:, :, f, :], hot_d[k][:, h * PAIR:(h + 1) * PAIR, :],
                                           part[:, bass.ds(g * GRP + h * PAIR, PAIR)].unsqueeze(2)
                                           .to_broadcast([P, PAIR, OHW]), ALU.mult).then_inc(hots_w, 1)

                def add_weights(g, h, first=False):
                    at = offsets(g, h)
                    pool.wait_ge(m_joined, g * 2 + h + 1)
                    for j in range(PAIR):
                        if first and h == 0 and j == 0:
                            pool.wait_ge(m_clear, 1)
                        else:
                            pool.wait_ge(m_added, g * GRP + h * PAIR + j)
                        part = M.rearrange("p b n -> p (b n)")[:, bass.ds(at[j], BN)]
                        pool.tensor_tensor(part, part, pair_w[h][:, j, 0, 0:BN], ALU.add).then_inc(m_added, 1)

                def group(g, k, second=False):
                    for h in range(2):
                        weigh(g, k, h)
                        add_weights(g - 1, h, first=second)

                weigh(0, 0, 0, first=True)
                weigh(0, 0, 1, first=True)
                pool.memset(M[:], 0.0).then_inc(m_clear, 1)
                group(1, 1, second=True)
                with pool.Fori(1, NGRP // 2) as it:
                    group(it * 2, 0)
                    group(it * 2 + 1, 1)
                for h in range(2):
                    add_weights(NGRP - 1, h)

            @block.tensor
            def _(pe):
                def spread(row, g):
                    pe.matmul(spread_ps[:], ident_b[0:NGRP, bass.ds(g, 1)].to_broadcast([NGRP, BN]), row[:],
                              start=True, stop=True).then_inc(spread_ready, 1)

                def sum_tile(g, j, k):
                    pe.wait_ge(lo_ready, g * GRP + j + 1)
                    sums = node_ps[j // PAIR]
                    pe.matmul(sums[:], hot_s[k][:, j, 0:BN], msg_hi[j][:], start=(j % PAIR == 0), stop=False)
                    pe.matmul(sums[:], hot_s[k][:, j, 0:BN], msg_lo[j][:], start=False,
                              stop=(j % PAIR == PAIR - 1)).then_inc(tile_summed, 1)

                def weights(g, k, h, first=False):
                    pe.wait_ge(hots_w, g * 4 + 2 * h + 2)
                    if not (first and h == 0):
                        pe.wait_ge(m_copied, g * 2 + h)
                    for j in range(PAIR):
                        mm = pe.matmul(m_ps[:, j], hot_s[k][:, h * PAIR + j, 0:BN], hot_w[h][:, j], start=True, stop=True)
                    mm.then_inc(m_ready, 1)

                def offsets(g):
                    _, at = nc.values_load_multi_w_load_instructions(
                        expand_at[0:1, bass.ds(g, 1), 0:GRP + 2].rearrange("p g j -> p (g j)"),
                        engines=[mybir.EngineType.PE], min_val=0, max_val=(NBLK - 1) * D,
                        skip_runtime_bounds_check_because=IN_RANGE)
                    return at

                def end_of_group(g, k):
                    sum_tile(g, 1, k)
                    weights(g - 1, 1 - k, 1)

                def group(g, k, at, first=False, second=False, last=False, load_next=False, whole=True):
                    at_next = None
                    for j in range(GRP):
                        a_rows = bass.ds(at[GRP + j // PAIR], D)
                        b_rows = bass.ds(at[j], D)
                        ts, td = turned_s[k][:, j * P:(j + 1) * P], turned_d[k][:, j * P:(j + 1) * P]
                        if j == 0:
                            pe.wait_ge(turned, g * 2 + 1)
                        pe.matmul(edge_ps[j][:], td, b_hi[:, b_rows], start=True, stop=False)
                        pe.matmul(edge_ps[j][:], td, b_lo[:, b_rows], start=False, stop=False)
                        if j == 0:
                            pe.wait_ge(turned, g * 2 + 2)
                        pe.matmul(edge_ps[j][:], ts, a_hi[:, a_rows], start=False, stop=False)
                        pe.matmul(edge_ps[j][:], ts, a_lo[:, a_rows], start=False, stop=True).then_inc(edge_ready, 1)
                        if j == 1 and load_next:
                            at_next = offsets(g + 1)
                        if j == 0 and not last:
                            pe.wait_ge(squared, g * 2 + 2)
                            spread(row_d, g + 1)
                        if j == 1 and not last:
                            pe.wait_ge(squared, g * 2 + 3)
                            spread(row_s, g + 1)
                        if j == 2:
                            sum_tile(g, 0, k)
                        elif j < 2 and not first:
                            sum_tile(g - 1, j + 2, 1 - k)
                        elif j == 3 and first:
                            sum_tile(g, 1, k)
                        if j == 1 and not first:
                            weights(g - 1, 1 - k, 0, first=second)
                    if whole and not first:
                        end_of_group(g, k)
                    return at_next

                for f, local in enumerate((local_d, local_s)):
                    for j in range(GRP):
                        mm = pe.transpose(edge_ps[f][0:NGRP, j * P:(j + 1) * P], local[:, j:NT:GRP], ident[:])
                    mm.then_inc(rows_ps, 1)
                pe.wait_ge(rows_out, 1)
                spread(row_d, 0)
                pe.wait_ge(rows_out, 2)
                pe.wait_ge(squared, 1)
                spread(row_s, 0)
                group(0, 0, offsets(0), first=True)
                group(1, 1, offsets(1), second=True, whole=False)
                with pe.Fori(0, (NGRP - 4) // UNROLL) as it:
                    at = offsets(it * UNROLL + 2)
                    end_of_group(it * UNROLL + 1, 1)
                    for i in range(UNROLL):
                        more = i < UNROLL - 1
                        at = group(it * UNROLL + 2 + i, i % 2, at, load_next=more, whole=more)
                at = offsets(NGRP - 2)
                end_of_group(NGRP - 3, 1)
                group(NGRP - 2, 0, at)
                group(NGRP - 1, 1, offsets(NGRP - 1), last=True)
                sum_tile(NGRP - 1, 2, 1)
                sum_tile(NGRP - 1, 3, 1)
                for h in range(2):
                    weights(NGRP - 1, 1, h)

            @block.scalar
            def _(act):
                def square_of(n):
                    act.wait_ge(spread_ready, n)
                    act.activation(square[:], spread_ps[:], ACT.Square, bias=minus_no[0:BN, :]).then_inc(squared, 1)

                def one_hot_of(n, hot):
                    act.wait_ge(squared, n)
                    act.activation(hot[:], square[:], ACT.Relu, bias=1.0, scale=-1.0).then_inc(turned, 1)

                def copy_weights(g, h, first=False):
                    act.wait_ge(m_ready, g * 2 + h + 1)
                    if not first:
                        act.wait_ge(m_added, g * GRP + h * PAIR - PAIR)
                    act.copy(pair_w[h][:], m_ps[:]).then_inc(m_copied, 1)

                def group(g, k, start=None, last=False):
                    for j in range(GRP):
                        act.wait_ge(edge_ready, g * GRP + j + 1)
                        act.activation(msg_hi[j][:], edge_ps[j][:], ACT.Relu).then_inc(hi_ready, 1)
                        if j == 0 and not last:
                            act.wait_ge(turned, g * 2 + 2)
                            square_of(g * 2 + 3)
                        if j == 0 and start not in (0, 1):
                            copy_weights(g - 2, 1, first=start == 2)
                        if j == 1 and not last:
                            one_hot_of(g * 2 + 3, turned_d[1 - k])
                            act.wait_ge(turned, g * 2 + 3)
                            square_of(g * 2 + 4)
                        if j == 2 and start != 0:
                            copy_weights(g - 1, 0, first=start == 1)
                        if j == 2 and not last:
                            one_hot_of(g * 2 + 4, turned_s[1 - k])

                for f, row in enumerate((row_d, row_s)):
                    act.wait_ge(rows_ps, f + 1)
                    act.copy(row[:], edge_ps[f][0:NGRP, :]).then_inc(rows_out, 1)
                square_of(1)
                one_hot_of(1, turned_d[0])
                act.wait_ge(turned, 1)
                square_of(2)
                one_hot_of(2, turned_s[0])
                for g in range(UNROLL + 2):
                    group(g, g % 2, start=g)
                with act.Fori(1, (NGRP - 4) // UNROLL) as it:
                    for i in range(UNROLL):
                        group(it * UNROLL + 2 + i, i % 2)
                group(NGRP - 2, 0)
                group(NGRP - 1, 1, last=True)
                copy_weights(NGRP - 2, 1)
                for h in range(2):
                    copy_weights(NGRP - 1, h)

            @block.vector
            def _(dve):
                def rows_of(g, h):
                    _, at = nc.values_load_multi_w_load_instructions(
                        gather_at[0:1, bass.ds(g, 1), GRP + h:GRP + h + 1].rearrange("p g j -> p (g j)"),
                        engines=[mybir.EngineType.DVE], min_val=0, max_val=(NBLK - 1) * D,
                        skip_runtime_bounds_check_because=IN_RANGE)
                    return bass.ds(at[0], D)

                def add_sums(g, h, first=False):
                    rows_at = rows_of(g, h)
                    dve.wait_ge(tile_summed, g * GRP + (h + 1) * PAIR)
                    if not first:
                        dve.wait_ge(node_added, g * 2 + h)
                    rows = S.rearrange("p b d -> p (b d)")[0:BN, rows_at]
                    dve.tensor_tensor(rows, rows, node_ps[h][:], ALU.add).then_inc(node_added, 1)

                def join_weights(g, h):
                    dve.wait_ge(m_copied, g * 2 + h + 1)
                    dve.tensor_tensor(pair_w[h][:, :, 0, :], pair_w[h][:, :, 0, :], pair_w[h][:, :, 1, :],
                                      ALU.add).then_inc(m_joined, 1)

                def make_hots(hot, local, g):
                    return dve.tensor_tensor(hot[:], iota[:, 1:1 + OHW].unsqueeze(1).to_broadcast([P, GRP, OHW]),
                                             local[:, bass.ds(g * GRP, GRP)].unsqueeze(2).to_broadcast([P, GRP, OHW]),
                                             ALU.is_equal)

                def group(g, k, start=None, last=False):
                    for j in range(GRP):
                        dve.wait_ge(hi_ready, g * GRP + j + 1)
                        dve.scalar_tensor_tensor(out=msg_lo[j][:], in0=edge_ps[j][:], scalar=0.0,
                                                 in1=msg_hi[j][:].bitcast(F32), op0=ALU.max,
                                                 op1=ALU.subtract).then_inc(lo_ready, 1)
                        if j == 1 and start != 0:
                            add_sums(g - 1, 1)
                            if start != 1:
                                join_weights(g - 2, 1)
                        if j == 2 and not last:
                            if start != 0:
                                dve.wait_ge(hots_w, g * 4)
                            make_hots(hot_d[1 - k], local_d, g + 1).then_inc(hots_d, 1)
                        if j == 3:
                            if not last:
                                if start != 0:
                                    dve.wait_ge(m_ready, g * 2)
                                make_hots(hot_s[1 - k], local_s, g + 1)
                            add_sums(g, 0, first=start == 0)
                            if start != 0:
                                join_weights(g - 1, 0)

                make_hots(hot_d[0], local_d, 0).then_inc(hots_d, 1)
                make_hots(hot_s[0], local_s, 0)
                group(0, 0, start=0)
                group(1, 1, start=1)
                with dve.Fori(0, (NGRP - 4) // UNROLL) as it:
                    for i in range(UNROLL):
                        group(it * UNROLL + 2 + i, i % 2)
                group(NGRP - 2, 0)
                group(NGRP - 1, 1, last=True)
                add_sums(NGRP - 1, 1)
                join_weights(NGRP - 2, 1)
                for h in range(2):
                    join_weights(NGRP - 1, h)

        psum_scope.close()
        scope.close()
        scope_ab.close()
        with ExitStack() as tail:
            def sb3(name, shape, dt):
                return sb(name, shape, dt, tail, "right")

            G = [sb3(f"G_{part}", [BN, NBLK, D], F32R) for part in ("hi", "lo")]
            w1_in = sb3("w1_in", [P, KC, D], F32)
            w1T = [sb3(f"w1T_{part}", [P, KC, D], F32R) for part in ("hi", "lo")]
            h2 = [sb3(f"h2_{k}", [BN, D], F32) for k in range(2)]
            h2T = [[sb3(f"h2T_{part}{k}", [P, KC, BN + 1], F32R) for part in ("hi", "lo")] for k in range(2)]
            M_d = [[sb3(f"M_{part}{k}", [BN, NBLK, BN + 1], F32R) for part in ("hi", "lo")] for k in range(2)]
            result = [sb3(f"result{k}", [BN, D], F32) for k in range(2)]
            neg_part = sb3("neg_part", [BN, D], F32)
            stats = sb3("stats", [BN, NBLK, nc.vector.BN_STATS_DIM], F32)
            mv = sb3("mv", [BN, NBLK, nc.vector.BN_AGGR_DIM], F32)
            std = sb3("std", [BN, NBLK], F32)
            psum = tail.enter_context(nc.psum_tensor("psum3", [P, 8, 512], F32))
            w1_loaded = sem("w1_loaded")
            stats_own = sem("stats_own")
            var_ready = sem("var_ready")
            std3 = sem("std3")
            rstd3 = sem("rstd3")
            h2_ready = sem("h2_ready")
            w1_ps = sem("w1_ps")
            w1_hi = sem("w1_hi")
            w1_lo = sem("w1_lo")
            h2_ps = sem("h2_ps")
            h2_hi = sem("h2_hi")
            h2_lo = sem("h2_lo")
            g_ps = sem("g_ps")
            g_hi = sem("g_hi")
            g_lo = sem("g_lo")
            m_hi = sem("m_hi")
            m_lo = sem("m_lo")
            out_ps = sem("out_ps")
            out_step = sem("out_step")
            out_ready = sem("out_ready")
            stored = [sem("stored0"), sem("stored1")]
            BATCHES = ((0, 2), (2, NBLK))
            W1_BANKS = (0, 1, 6, 7)

            def blocks_of_m(d):
                return M[:].rearrange("p (s d) n -> p s d n", d=NBLK)[:, :, d, :]

            with nc.Block() as block:
                @block.sync
                def _(sp):
                    sp.dma_start(w1_in[:], w1.rearrange("(o p) i -> p o i", p=P)).then_inc(w1_loaded, 16)
                    for b in range(NBLK):
                        sp.wait_ge(out_ready, b + 1)
                        sp.dma_start(out[b * BN:(b + 1) * BN, :], result[b % 2][:]).then_inc(stored[b % 2], 16)
                    for k in range(2):
                        sp.wait_ge(stored[k], 16 * (NBLK // 2))

                @block.vector
                def _(dve):
                    def rest(b):
                        lo, hi = BATCHES[b]
                        dve.wait_ge(std3, b + 1)
                        dve.reciprocal(rstd[0:BN, lo:hi], std[:, lo:hi]).then_inc(rstd3, 1)
                        dve.wait_ge(rstd3, 2 * b + 1)
                        dve.scalar_tensor_tensor(out=shift[0:BN, lo:hi], in0=mv[:, lo:hi, 0], scalar=-1.0,
                                                 in1=rstd[0:BN, lo:hi], op0=ALU.mult, op1=ALU.mult).then_inc(rstd3, 1)

                    def low_of(out, value, high, done):
                        dve.tensor_tensor(out, value, high.bitcast(F32), ALU.subtract).then_inc(done, 1)

                    def low_of_h2(b):
                        dve.wait_ge(h2_hi, b + 1)
                        low_of(h2T[b % 2][1][:, :, 0:BN], psum[:, 2 + b % 2, 0:KC * BN].rearrange("p (c n) -> p c n", c=KC),
                               h2T[b % 2][0][:, :, 0:BN], h2_lo)

                    def low_of_w1(i):
                        dve.wait_ge(w1_hi, i + 1)
                        low_of(w1T[1][:, i, :], psum[:, W1_BANKS[i], :], w1T[0][:, i, :], w1_lo)

                    for b, (lo, hi) in enumerate(BATCHES):
                        for n in range(lo, hi):
                            dve.bn_stats(stats[:, n, :], S[0:BN, n, :]).then_inc(stats_own, 1)
                            if n == 3:
                                rest(0)
                        for n in range(lo, hi):
                            dve.wait_ge(stats_own, n + 1)
                            dve.bn_aggr(mv[:, n, :], stats[:, n, :]).then_inc(var_ready, 1)
                    for b in range(2):
                        low_of_h2(b)
                    for i in range(KC):
                        low_of_w1(i)
                    rest(1)

                    def low_of_m(d):
                        dve.wait_ge(m_hi, d + 1)
                        if d >= 2:
                            dve.wait_ge(out_ps, d - 1)
                        low_of(M_d[d % 2][1][:, :, 0:BN], blocks_of_m(d), M_d[d % 2][0][:, :, 0:BN], m_lo)

                    for b in range(NBLK):
                        if b >= 2:
                            dve.wait_ge(g_ps, b - 1)
                            low_of_h2(b)
                        if b >= 1:
                            dve.wait_ge(g_hi, b)
                            low_of(G[1][:, b - 1, :], psum[0:BN, 4 + (b - 1) % 2, :], G[0][:, b - 1, :], g_lo)
                    low_of_m(0)
                    dve.wait_ge(g_hi, NBLK)
                    low_of(G[1][:, NBLK - 1, :], psum[0:BN, 4 + (NBLK - 1) % 2, :], G[0][:, NBLK - 1, :], g_lo)
                    low_of_m(1)
                    for b in range(NBLK):
                        o = psum[0:BN, (6 + b) % 8, :]
                        res = result[b % 2]
                        dve.wait_ge(out_ps, b + 1)
                        if b + 2 < NBLK:
                            low_of_m(b + 2)
                        if b >= 2:
                            dve.wait_ge(stored[b % 2], 16 * (b // 2))
                        if b >= 1:
                            dve.wait_ge(out_ready, b)
                        dve.tensor_scalar(neg_part[:], o, 0.0, alpha_t[0:BN, :], ALU.min, ALU.mult).then_inc(out_step, 1)
                        dve.wait_ge(out_step, 2 * b + 1)
                        dve.scalar_tensor_tensor(out=res[:], in0=o, scalar=0.0, in1=neg_part[:], op0=ALU.max,
                                                 op1=ALU.add).then_inc(out_step, 1)
                        dve.wait_ge(out_step, 2 * b + 2)
                        dve.tensor_tensor(res[:], res[:], S[0:BN, b, :], ALU.add).then_inc(out_ready, 1)

                @block.scalar
                def _(act):
                    def deviation(b):
                        lo, hi = BATCHES[b]
                        act.wait_ge(var_ready, hi)
                        act.activation(std[:, lo:hi], mv[:, lo:hi, 1], ACT.Sqrt, bias=eps_t[0:BN, :]).then_inc(std3, 1)

                    def normal(b):
                        act.activation(h2[b % 2][:], S[0:BN, b, :], ACT.Relu, bias=shift[0:BN, b:b + 1],
                                       scale=rstd[0:BN, b:b + 1]).then_inc(h2_ready, 1)

                    def high_of_m(d):
                        act.copy(M_d[d % 2][0][:, :, 0:BN], blocks_of_m(d)).then_inc(m_hi, 1)

                    def high_of_h2(b):
                        act.wait_ge(h2_ps, b + 1)
                        act.copy(h2T[b % 2][0][:, :, 0:BN],
                                 psum[:, 2 + b % 2, 0:KC * BN].rearrange("p (c n) -> p c n", c=KC)).then_inc(h2_hi, 1)

                    deviation(0)
                    act.wait_ge(rstd3, 2)
                    normal(0)
                    normal(1)
                    high_of_h2(0)
                    high_of_h2(1)
                    for i in range(KC):
                        act.wait_ge(w1_ps, i + 1)
                        act.copy(w1T[0][:, i, :], psum[:, W1_BANKS[i], :]).then_inc(w1_hi, 1)
                    deviation(1)
                    act.wait_ge(rstd3, 4)
                    for b in range(NBLK):
                        if b >= 2:
                            act.wait_ge(g_ps, b - 1)
                            high_of_h2(b)
                        if b + 2 < NBLK:
                            normal(b + 2)
                        if b >= 1:
                            act.wait_ge(g_ps, b)
                            act.copy(G[0][:, b - 1, :], psum[0:BN, 4 + (b - 1) % 2, :]).then_inc(g_hi, 1)
                    high_of_m(0)
                    act.wait_ge(g_ps, NBLK)
                    act.copy(G[0][:, NBLK - 1, :], psum[0:BN, 4 + (NBLK - 1) % 2, :]).then_inc(g_hi, 1)
                    high_of_m(1)
                    for d in range(2, NBLK):
                        act.wait_ge(out_ps, d - 1)
                        high_of_m(d)

                @block.tensor
                def _(pe):
                    def product(ps, stationary, moving, first, last):
                        pe.matmul(ps, stationary[0], moving[0], start=first, stop=False)
                        pe.matmul(ps, stationary[1], moving[0], start=False, stop=False)
                        return pe.matmul(ps, stationary[0], moving[1], start=False, stop=last)

                    def turn(b):
                        pe.wait_ge(h2_ready, b + 1)
                        if b >= 2:
                            pe.wait_ge(h2_lo, b - 1)
                        for c in range(KC):
                            mm = pe.transpose(psum[:, 2 + b % 2, c * BN:(c + 1) * BN], h2[b % 2][:, c * P:(c + 1) * P],
                                              ident[0:BN, 0:BN])
                        mm.then_inc(h2_ps, 1)

                    turn(0)
                    turn(1)
                    pe.wait_ge(w1_loaded, 16)
                    for i in range(KC):
                        for o in range(KC):
                            mm = pe.transpose(psum[:, W1_BANKS[i], o * P:(o + 1) * P], w1_in[:, o, i * P:(i + 1) * P], ident[:])
                        mm.then_inc(w1_ps, 1)
                    pe.wait_ge(w1_lo, KC)
                    for b in range(NBLK):
                        if b >= 1 and b + 1 < NBLK:
                            turn(b + 1)
                        pe.wait_ge(h2_lo, b + 1)
                        if b >= 2:
                            pe.wait_ge(g_lo, b - 1)
                        for c in range(KC):
                            mm = product(psum[0:BN, 4 + b % 2, :], [part[:, c, 0:BN] for part in h2T[b % 2]],
                                         [part[:, c, :] for part in w1T], c == 0, c == KC - 1)
                        mm.then_inc(g_ps, 1)
                    for d in range(NBLK):
                        pe.wait_ge(m_lo, d + 1)
                        if d >= 8:
                            pe.wait_ge(out_step, 2 * (d - 8) + 2)
                        for s in range(NBLK):
                            if d == 0:
                                pe.wait_ge(g_lo, s + 1)
                            mm = product(psum[0:BN, (6 + d) % 8, :], [part[:, s, 0:BN] for part in M_d[d % 2]],
                                         [part[:, s, :] for part in G], s == 0, s == NBLK - 1)
                        mm.then_inc(out_ps, 1)
        scope_m.close()


_INS = ['x', 'src', 'dst', 'edge_weight', 'L0_gnn_W', 'L0_gnn_b', 'L1_gnn_W', 'L1_gnn_alpha']


def kernel(**inputs):
    import numpy as _np
    import concourse.bacc as _bacc
    from concourse import mybir as _mybir
    from concourse.bass_utils import run_bass_kernel_spmd as _run

    nc = _bacc.Bacc("TRN2", target_bir_lowering=False, num_devices=1)
    arrays, args = {}, []
    for name in _INS:
        a = _np.ascontiguousarray(inputs[name])
        arrays[f"in_{name}_dram"] = a
        args.append(nc.dram_tensor(f"in_{name}_dram", a.shape, _mybir.dt.from_np(a.dtype), kind="ExternalInput").ap())
    out = nc.dram_tensor("out_dram", (N, D), F32, kind="ExternalOutput").ap()
    build(nc, *args, out)
    r = _run(nc, [arrays], core_ids=[0])
    return r.results[0]["out_dram"]
```
